# Optimizing a Trainium2 kernel written in Bass

```python
import numpy as np
import jax
import jax.numpy as jnp

def _softmax(x, axis=-1):
    return jax.nn.softmax(x, axis=axis)

def _gelu(x):
    return jax.nn.gelu(x, approximate=True)

def _silu(x):
    return jax.nn.silu(x)

def _sigmoid(x):
    return jax.nn.sigmoid(x)

def _layernorm(x, axis=-1, eps=1e-05):
    m = jnp.mean(x, axis=axis, keepdims=True)
    v = jnp.var(x, axis=axis, keepdims=True)
    return (x - m) / jnp.sqrt(v + eps)

def _scatter_add(tgt, idx, src, axis=0):
    return tgt.at[idx].add(src)

def _segment_sum(src, seg, n):
    return jax.ops.segment_sum(src, seg, n)
kernel_name = 'mk_adj_resnorm_d4_adj_r2_911a40'

def setup_inputs(seed: int=0):
    np.random.seed(seed)
    _w = jnp.asarray

    def _rec_inputs():
        import jax
        import jax.numpy as jnp
        _gk = jax.random.key(seed)
        x = -0.0002928 + 1 * jax.random.normal(jax.random.fold_in(_gk, 1), (64, 128, 128), jnp.float32)
        _a = jax.random.bernoulli(jax.random.fold_in(_gk, 2), 0.0625, (64, 128, 128))
        adj = _a.astype(jnp.int32)
        return (x, adj)
    x, adj = _rec_inputs()

    def _L0_gnn_setup():
        import jax, jax.numpy as jnp
        import numpy as np
        OUT = 128
        NUM_LAYERS = 3

        def _gru_cell(inp, h, w_ih, w_hh, b_ih, b_hh):
            gi = inp @ w_ih.T + b_ih
            gh = h @ w_hh.T + b_hh
            i_r, i_z, i_n = jnp.split(gi, 3, axis=-1)
            h_r, h_z, h_n = jnp.split(gh, 3, axis=-1)
            r = jax.nn.sigmoid(i_r + h_r)
            z = jax.nn.sigmoid(i_z + h_z)
            n = jnp.tanh(i_n + r * h_n)
            return (1.0 - z) * n + z * h
        key = jax.random.key(seed)
        ks = jax.random.split(key, 8)
        B, N, D = (32, 256, 128)
        x = jax.random.normal(ks[0], (B, N, D), dtype=jnp.float32)
        adj = jax.random.randint(ks[1], (B, N, N), 0, 2, dtype=jnp.int32)
        s = 1.0 / np.sqrt(OUT)
        weight = jax.random.uniform(ks[2], (NUM_LAYERS, OUT, OUT), jnp.float32, -s, s)
        w_ih = jax.random.uniform(ks[3], (3 * OUT, OUT), jnp.float32, -s, s)
        w_hh = jax.random.uniform(ks[4], (3 * OUT, OUT), jnp.float32, -s, s)
        b_ih = jax.random.uniform(ks[5], (3 * OUT,), jnp.float32, -s, s)
        b_hh = jax.random.uniform(ks[6], (3 * OUT,), jnp.float32, -s, s)
        return {'x': x, 'adj': adj, 'weight': weight, 'w_ih': w_ih, 'w_hh': w_hh, 'b_ih': b_ih, 'b_hh': b_hh}
    _L0_gnn_all = _L0_gnn_setup()
    _L0_gnn_in = {k: v for k, v in _L0_gnn_all.items() if k in ('weight', 'w_ih', 'w_hh', 'b_ih', 'b_hh')}
    del _L0_gnn_all

    def _L1_gnn_setup():
        import jax, jax.numpy as jnp
        import numpy as np
        NEG_INF = -9000000000000000.0
        ALPHA = 0.2
        key = jax.random.key(seed)
        k1, k2, k3, k4 = jax.random.split(key, 4)
        B, N, C_IN, C_OUT, H = (8, 1024, 128, 128, 4)
        node_feats = jax.random.normal(k1, (B, N, C_IN), dtype=jnp.float32)
        adj_matrix = jax.random.randint(k2, (B, N, N), 0, 2, dtype=jnp.int32)
        eye = jnp.eye(N, dtype=jnp.int32)[None]
        adj_matrix = jnp.maximum(adj_matrix, eye)
        W = jax.random.normal(k3, (C_OUT, C_IN), dtype=jnp.float32) * (1.414 / np.sqrt(C_IN))
        b = jnp.zeros((C_OUT,), dtype=jnp.float32)
        a = jax.random.normal(k4, (H, 2 * (C_OUT // H)), dtype=jnp.float32) * 0.1
        return {'node_feats': node_feats, 'adj_matrix': adj_matrix, 'W': W, 'b': b, 'a': a}
    _L1_gnn_all = _L1_gnn_setup()
    _L1_gnn_in = {k: v for k, v in _L1_gnn_all.items() if k in ('W', 'b', 'a')}
    del _L1_gnn_all

    def _L2_gnn_setup():
        import jax, jax.numpy as jnp
        import numpy as np
        NEG_INF = -9000000000000000.0
        LEAKY_SLOPE = 0.2
        key = jax.random.key(seed)
        k1, k2, k3, k4, k5, k6 = jax.random.split(key, 6)
        B, N, D = (256, 200, 128)
        hidden = jax.random.normal(k1, (B, N, D), dtype=jnp.float32)
        adj = jax.random.randint(k2, (B, N, N), 0, 5, dtype=jnp.int32)
        a0 = jax.random.normal(k3, (D,), dtype=jnp.float32)
        a1 = jax.random.normal(k4, (D,), dtype=jnp.float32)
        a2 = jax.random.normal(k5, (D,), dtype=jnp.float32)
        a3 = jax.random.normal(k6, (D,), dtype=jnp.float32)
        return {'hidden': hidden, 'adj': adj, 'a0': a0, 'a1': a1, 'a2': a2, 'a3': a3}
    _L2_gnn_all = _L2_gnn_setup()
    _L2_gnn_in = {k: v for k, v in _L2_gnn_all.items() if k in ('a0', 'a1', 'a2', 'a3')}
    del _L2_gnn_all

    def _L3_gnn_setup():
        import jax, jax.numpy as jnp
        import numpy as np
        B, S, DIN, DOUT = (8, 1024, 128, 128)
        ALPHA = 0.2
        NEG = -9000000000000000.0
        key = jax.random.key(seed)
        k1, k2, k3, k4 = jax.random.split(key, 4)
        x = jax.random.normal(k1, (B, S, DIN), dtype=jnp.float32)
        adj = jax.random.randint(k2, (B, S, S), 0, 2, dtype=jnp.int32)
        limW = float(np.sqrt(6.0 / (DIN + DOUT)))
        lima = float(np.sqrt(6.0 / (2 * DOUT + 1)))
        W = jax.random.uniform(k3, (DOUT, DIN), jnp.float32, -limW, limW)
        a = jax.random.uniform(k4, (1, 2 * DOUT), jnp.float32, -lima, lima)
        return {'x': x, 'adj': adj, 'W': W, 'a': a}
    _L3_gnn_all = _L3_gnn_setup()
    _L3_gnn_in = {k: v for k, v in _L3_gnn_all.items() if k in ('W', 'a')}
    del _L3_gnn_all
    return {'x': x, 'adj': adj, 'L0_gnn_weight': _L0_gnn_in['weight'], 'L0_gnn_w_ih': _L0_gnn_in['w_ih'], 'L0_gnn_w_hh': _L0_gnn_in['w_hh'], 'L0_gnn_b_ih': _L0_gnn_in['b_ih'], 'L0_gnn_b_hh': _L0_gnn_in['b_hh'], 'L1_gnn_W': _L1_gnn_in['W'], 'L1_gnn_b': _L1_gnn_in['b'], 'L1_gnn_a': _L1_gnn_in['a'], 'L2_gnn_a0': _L2_gnn_in['a0'], 'L2_gnn_a1': _L2_gnn_in['a1'], 'L2_gnn_a2': _L2_gnn_in['a2'], 'L2_gnn_a3': _L2_gnn_in['a3'], 'L3_gnn_W': _L3_gnn_in['W'], 'L3_gnn_a': _L3_gnn_in['a']}

def reference(x, adj, L0_gnn_weight, L0_gnn_w_ih, L0_gnn_w_hh, L0_gnn_b_ih, L0_gnn_b_hh, L1_gnn_W, L1_gnn_b, L1_gnn_a, L2_gnn_a0, L2_gnn_a1, L2_gnn_a2, L2_gnn_a3, L3_gnn_W, L3_gnn_a):
    import jax
    import jax.numpy as jnp

    def _L0_gnn_ref(x, adj, weight, w_ih, w_hh, b_ih, b_hh):
        import jax, jax.numpy as jnp
        import numpy as np
        OUT = 128
        NUM_LAYERS = 3

        def _gru_cell(inp, h, w_ih, w_hh, b_ih, b_hh):
            gi = inp @ w_ih.T + b_ih
            gh = h @ w_hh.T + b_hh
            i_r, i_z, i_n = jnp.split(gi, 3, axis=-1)
            h_r, h_z, h_n = jnp.split(gh, 3, axis=-1)
            r = jax.nn.sigmoid(i_r + h_r)
            z = jax.nn.sigmoid(i_z + h_z)
            n = jnp.tanh(i_n + r * h_n)
            return (1.0 - z) * n + z * h
        A = (adj != 0).astype(x.dtype)
        h = x
        L = weight.shape[0]
        for i in range(L):
            m = jnp.einsum('bnd,de->bne', h, weight[i])
            aggr = jnp.einsum('bst,bsd->btd', A, m)
            h = _gru_cell(aggr, h, w_ih, w_hh, b_ih, b_hh)
        return h

    def _L1_gnn_ref(node_feats, adj_matrix, W, b, a):
        import jax, jax.numpy as jnp
        import numpy as np
        NEG_INF = -9000000000000000.0
        ALPHA = 0.2
        B, N, _ = node_feats.shape
        H, two_c = a.shape
        c = two_c // 2
        f = (jnp.einsum('bni,oi->bno', node_feats, W) + b).reshape(B, N, H, c)
        a_src, a_dst = (a[:, :c], a[:, c:])
        s_src = jnp.einsum('bnhc,hc->bnh', f, a_src)
        s_dst = jnp.einsum('bnhc,hc->bnh', f, a_dst)
        logits = jax.nn.leaky_relu(s_src[:, :, None, :] + s_dst[:, None, :, :], ALPHA)
        logits = jnp.where(adj_matrix[..., None] == 1, logits, NEG_INF)
        probs = jax.nn.softmax(logits, axis=2)
        out = jnp.einsum('bijh,bjhc->bihc', probs, f)
        return out.reshape(B, N, H * c)

    def _L2_gnn_ref(hidden, adj, a0, a1, a2, a3):
        import jax, jax.numpy as jnp
        import numpy as np
        NEG_INF = -9000000000000000.0
        LEAKY_SLOPE = 0.2

        def edge_score(a):
            s = jnp.einsum('bid,bjd->bij', hidden * a, hidden)
            return jax.nn.leaky_relu(s, LEAKY_SLOPE)
        e0, e1, e2, e3 = (edge_score(a0), edge_score(a1), edge_score(a2), edge_score(a3))
        alpha = jnp.where(adj == 1, e0, NEG_INF)
        alpha = jnp.where(adj == 2, e1, alpha)
        alpha = jnp.where(adj == 3, e2, alpha)
        alpha = jnp.where(adj == 4, e3, alpha)
        alpha = jax.nn.softmax(alpha, axis=-1)
        return jnp.matmul(alpha, hidden)

    def _L3_gnn_ref(x, adj, W, a):
        import jax, jax.numpy as jnp
        import numpy as np
        B, S, DIN, DOUT = (8, 1024, 128, 128)
        ALPHA = 0.2
        NEG = -9000000000000000.0
        h = jnp.einsum('bsf,of->bso', x, W)
        a1 = a[0, :DOUT]
        a2 = a[0, DOUT:]
        f_i = h @ a1
        f_j = h @ a2
        e = f_i[:, :, None] + f_j[:, None, :]
        e = jnp.where(e >= 0, e, ALPHA * e)
        att = jnp.where(adj > 0, e, NEG)
        att = jax.nn.softmax(att, axis=2)
        h_prime = jnp.einsum('bij,bjo->bio', att, h)
        return h_prime
    x = _layernorm(x + _L0_gnn_ref(x, adj, L0_gnn_weight, L0_gnn_w_ih, L0_gnn_w_hh, L0_gnn_b_ih, L0_gnn_b_hh), axis=-1)
    x = _layernorm(x + _L1_gnn_ref(x, adj, L1_gnn_W, L1_gnn_b, L1_gnn_a), axis=-1)
    x = _layernorm(x + _L2_gnn_ref(x, adj, L2_gnn_a0, L2_gnn_a1, L2_gnn_a2, L2_gnn_a3), axis=-1)
    x = _layernorm(x + _L3_gnn_ref(x, adj, L3_gnn_W, L3_gnn_a), axis=-1)
    return x

_drawn_inputs = setup_inputs


def setup_inputs(seed=0):
    import zlib

    import numpy as np

    out = dict(_drawn_inputs(seed))
    spreads = {'L1_gnn_b': (0.0, 0.1)}
    factors = {}
    for name, (base, spread) in spreads.items():
        noise = np.random.default_rng([zlib.crc32(name.encode()), seed]).standard_normal(out[name].shape)
        drawn = base * np.exp(spread * noise) if base else spread * noise
        out[name] = jnp.asarray(drawn.astype(out[name].dtype))
    for name, factor in factors.items():
        out[name] = (out[name] * factor).astype(out[name].dtype)
    return out
```

```python
from contextlib import ExitStack

import concourse.bass as bass
from concourse import mybir

F32 = mybir.dt.float32
F32R = mybir.dt.float32r
BF16 = mybir.dt.bfloat16
I32 = mybir.dt.int32
ALU = mybir.AluOpType
ACT = mybir.ActivationFunctionType
AX = mybir.AxisListType

P = 128
G = 4
W = G * P
XS = (0, 1)
EPS = 1e-5
SLOPE = 0.2
BIG = 2.0 ** 100


def at(it, per, k):
    return it * per + k


def program(nc, x, adj, ggnn_w, w_ih, w_hh, b_ih, b_hh, gat_w, gat_b, gat_a, edge_a, one_w, one_a, out):
    B, N, D = x.shape
    L = ggnn_w.shape[0]
    H = gat_a.shape[0]
    C = D // H
    K = len(edge_a)
    PAIRS = B // (2 * G)
    U = H + 2
    UE, UO = H, H + 1
    assert N == P and D == P and B % (2 * G) == 0 and K == 4 and H == 4

    with ExitStack() as ctx:
        def sb(name, shape, dt=F32):
            return ctx.enter_context(nc.sbuf_tensor(name, shape, dt))

        def sem(name):
            return ctx.enter_context(nc.semaphore(name))

        def sems(name):
            return [sem(f"{name}_{g}") for g in "ab"]

        ctx.enter_context(nc.allow_non_contiguous_dma(reason="small columns of biases and vectors"))

        bank = [ctx.enter_context(nc.psum_tensor(f"bank_{g}", [P, 4, W], F32)) for g in "ab"]

        ident = sb("ident", [P, P])
        ident_r = sb("ident_r", [P, P], F32R)
        big_ident = sb("big_ident", [P, P], BF16)
        w_raw = sb("w_raw", [P, 3 * 2 + L + 2, P])
        w_t = sb("w_t", [P, 3 * 2 + L + 2, P])
        cw_hi = sb("cw_hi", [P, L, 3 * P], F32R)
        cw_lo = sb("cw_lo", [P, L, 3 * P], F32R)
        hw_hi = sb("hw_hi", [P, 3 * P], F32R)
        hw_lo = sb("hw_lo", [P, 3 * P], F32R)
        b_ih_c = sb("b_ih_c", [P, 3])
        b_hh_c = sb("b_hh_c", [P, 3])
        b_gate = sb("b_gate", [P, 3])
        nb_z = sb("nb_z", [P, 1])
        a_src = sb("a_src", [P, 1])
        a_dst = sb("a_dst", [P, 1])
        a_sum = sb("a_sum", [P, 1])
        gat_b_c = sb("gat_b_c", [P, 1])
        one_a_c = sb("one_a_c", [P, 2])
        edge_a_c = sb("edge_a_c", [P, K])
        a_wide = sb("a_wide", [P, 3, H, P])
        b_wide = sb("b_wide", [P, P])
        one_wide = sb("one_wide", [P, 2, P])
        b_diag = sb("b_diag", [P, P])
        ones = sb("ones", [P, P])
        v_src = sb("v_src", [P, H, P])
        v_dst = sb("v_dst", [P, H, P])
        v_one = sb("v_one", [P, 2, P])
        c_head = sb("c_head", [P, H])
        c_head_s = sb("c_head_s", [P, H])
        b_row = sb("b_row", [P, P])
        eps = sb("eps", [P, G])
        minus_half = sb("minus_half", [P, G])

        y_all = sb("y_all", [P, B * D])

        x_in = sb("x_in", [P, 2, W])
        adj_in = sb("adj_in", [P, 2, W], I32)
        edges = sb("edges", [P, 2, W], F32R)
        typ_in = adj_in
        mask = sb("mask", [P, 2, K + 1, W], BF16)
        y = sb("y", [P, 2, W])
        stats = sb("stats", [P, 2, 4, G, 6])
        tick = sb("tick", [P, 1])
        mv = sb("mv", [P, 2, 4, G, 2])
        ve = sb("ve", [P, 2, 4, G])
        rstd = sb("rstd", [P, 2, 4, G])
        nmr = sb("nmr", [P, 2, 4, G])
        x1 = sb("x1", [P, 2, W])
        x1b = sb("x1b", [P, 2, W])
        x2 = sb("x2", [P, 2, G, P + 1])
        x3 = sb("x3", [P, 2, W])
        x4 = sb("x4", [P, 2, W])
        x_t = sb("x_t", [P, 2, W])
        f1 = sb("f1", [P, 2, G, H, C + 1])
        f3 = sb("f3", [P, 2, G, P + 1])
        top = sb("top", [P, 2, U, G])
        rden = sb("rden", [P, 2, 3, H * G])

        with ExitStack() as part_1:
            def sb_1(name, shape, dt=F32):
                return part_1.enter_context(nc.sbuf_tensor(name, shape, dt))

            h_t = sb_1("h_t", [P, 2, W])
            h_hi = sb_1("h_hi", [P, 2, W], F32R)
            h_lo = sb_1("h_lo", [P, 2, W], F32R)
            hn_hi = sb_1("hn_hi", [P, 2, W], F32R)
            hn_lo = sb_1("hn_lo", [P, 2, W], F32R)
            q_hi = sb_1("q_hi", [P, 2, W], F32R)
            q_lo = sb_1("q_lo", [P, 2, W], F32R)
            r_g = sb_1("r_g", [P, 2, W])
            z_g = sb_1("z_g", [P, 2, W])
            nz_g = sb_1("nz_g", [P, 2, W])
            zh = sb_1("zh", [P, 2, W])
            rn = sb_1("rn", [P, 2, W])
            npre = sb_1("npre", [P, 2, W])
            n_g = sb_1("n_g", [P, 2, W])
            nzn = sb_1("nzn", [P, 2, W])
        xs_t = sb("xs_t", [P, 2, K, W])
        scaled = sb("scaled", [P, 2, 2, W])
        score = sb("score", [P, 2, H, W])
        prob_t = sb("prob_t", [P, 2, H, W])

        raw_in = sem("raw_in")
        const_pool = sem("const_pool")
        const_dve = sem("const_dve")
        const_pe = sem("const_pe")
        const_act = sem("const_act")
        chain_sem = sem("chain_sem")

        x_loaded = sem("x_loaded")
        adj_loaded = sem("adj_loaded")
        resid_loaded = sem("resid_loaded")
        edges_ready = sems("edges_ready")
        tr_ready = sems("tr_ready")
        ht_copied = sems("ht_copied")
        h_hi_ready = sems("h_hi_ready")
        h_lo_ready = sems("h_lo_ready")
        hn_hi_ready = sems("hn_hi_ready")
        hn_lo_ready = sems("hn_lo_ready")
        q_ready = sems("q_ready")
        q_hi_ready = sems("q_hi_ready")
        q_lo_ready = sems("q_lo_ready")
        gates_ready = sems("gates_ready")
        r_ready = sems("r_ready")
        z_ready = sems("z_ready")
        nz_ready = sems("nz_ready")
        rn_ready = sems("rn_ready")
        npre_ready = sems("npre_ready")
        n_ready = sems("n_ready")
        zh_ready = sems("zh_ready")
        nzn_ready = sems("nzn_ready")
        h_new = sems("h_new")
        y_stored = sems("y_stored")

        typ_loaded = sem("typ_loaded")
        masks_ready = sems("masks_ready")
        stats_ready = sems("stats_ready")
        mv_ready = sems("mv_ready")
        ve_ready = sems("ve_ready")
        rstd_ready = sems("rstd_ready")
        nmr_ready = sems("nmr_ready")
        x_normed = sems("x_normed")
        x1b_ready = sems("x1b_ready")
        xt_ready = sems("xt_ready")
        xt_copied = sems("xt_copied")
        xs_ready = sems("xs_ready")
        f_ready = sems("f_ready")
        f_copied = sems("f_copied")
        u_ready = sems("u_ready")
        t_ready = sems("t_ready")
        v_ready = sems("v_ready")
        top_ready = sems("top_ready")
        sub_ready = sems("sub_ready")
        p_ready = sems("p_ready")
        pt_ready = sems("pt_ready")
        pt_copied = sems("pt_copied")
        e_ready = sems("e_ready")
        o_ready = sems("o_ready")
        rden_ready = sems("rden_ready")
        o_scaled = sems("o_scaled")
        y_ready = sems("y_ready")
        out_stored = sem("out_stored")

        def g4(ap):
            return ap.rearrange("p (g n) -> p g n", g=G)

        def cols(g):
            return slice(g * P, (g + 1) * P)

        def y_at(it, X):
            return y_all[:, bass.ds(it * (2 * W) + X * W, W)]

        def y_graph(it, X, g):
            return y_all[:, bass.ds(it * (2 * W) + X * W + g * P, P)]

        def pair_of(dram, it):
            return dram[bass.ds(it * (2 * G), 2 * G), :, :].rearrange("b n d -> n b d")

        def both(tile):
            return tile[:, :, :].rearrange("p x (g n) -> p (x g) n", g=G)

        blocks = ([w_ih[P * i:P * i + P, :] for i in range(3)] + [w_hh[P * i:P * i + P, :] for i in range(3)]
                  + [ggnn_w[i] for i in range(L)] + [gat_w, one_w])
        I_IH, I_HH, I_W, I_GAT, I_ONE = 0, 3, 6, 6 + L, 7 + L
        NW = len(blocks)
        N_RAW = NW + 2 + 2 * H + 1 + 1 + K

        block = ctx.enter_context(nc.Block())

        @block.sync
        def _(sp):
            for i, w in enumerate(blocks):
                sp.dma_start(w_raw[:, i, :], w).then_inc(raw_in, 16)
            sp.dma_start(b_ih_c[:, :], b_ih.rearrange("(g o) -> o g", g=3)).then_inc(raw_in, 16)
            sp.dma_start(b_hh_c[:, :], b_hh.rearrange("(g o) -> o g", g=3)).then_inc(raw_in, 16)
            for h in range(H):
                rows = slice(h * C, (h + 1) * C)
                sp.dma_start(a_src[rows, :], gat_a[h, 0:C].rearrange("(c o) -> c o", o=1)).then_inc(raw_in, 16)
                sp.dma_start(a_dst[rows, :], gat_a[h, C:2 * C].rearrange("(c o) -> c o", o=1)).then_inc(raw_in, 16)
            sp.dma_start(gat_b_c[:, :], gat_b.rearrange("(c o) -> c o", o=1)).then_inc(raw_in, 16)
            sp.dma_start(one_a_c[:, :], one_a.rearrange("a (s c) -> c (a s)", s=2)).then_inc(raw_in, 16)
            for k in range(K):
                sp.dma_start(edge_a_c[:, k:k + 1], edge_a[k].rearrange("(c o) -> c o", o=1)).then_inc(raw_in, 16)

            def load_pair(it):
                sp.dma_start(both(x_in), pair_of(x, it)).then_inc(x_loaded, 16)
                sp.dma_start(both(adj_in), pair_of(adj, it)).then_inc(adj_loaded, 16)
                sp.dma_start(y_all[:, bass.ds(it * (2 * W), 2 * W)].rearrange("p (b d) -> p b d", d=D),
                             pair_of(x, it)).then_inc(resid_loaded, 16)

            load_pair(0)
            with sp.Fori(1, PAIRS) as it:
                for X in XS:
                    sp.wait_ge(tr_ready[X], at(it - 1, L + 1, 1))
                    sp.wait_ge(hn_lo_ready[X], at(it - 1, L, 1))
                    sp.wait_ge(edges_ready[X], it)
                sp.wait_ge(resid_loaded, at(it - 1, 16, 16))
                load_pair(it)

            for X in XS:
                sp.wait_ge(edges_ready[X], PAIRS)
            sp.dma_start(both(typ_in), pair_of(adj, 0)).then_inc(typ_loaded, 16)
            with sp.Fori(1, PAIRS) as it:
                for X in XS:
                    sp.wait_ge(masks_ready[X], it)
                sp.dma_start(both(typ_in), pair_of(adj, it)).then_inc(typ_loaded, 16)
                for X in XS:
                    sp.wait_ge(x_normed[X], at(it - 1, 4, 4))
                sp.dma_start(pair_of(out, it - 1), both(x4)).then_inc(out_stored, 16)
            for X in XS:
                sp.wait_ge(x_normed[X], PAIRS * 4)
            sp.dma_start(pair_of(out, PAIRS - 1), both(x4)).then_inc(out_stored, 16)
            sp.wait_ge(out_stored, 16 * (PAIRS + 1))

        @block.gpsimd
        def _(pool):
            nc.gpsimd.memset(ident[:, :], 1.0).then_inc(const_pool, 1)
            pool.wait_ge(const_pool, 1)
            nc.gpsimd.affine_select(out=ident[:, :], in_=ident[:, :], compare_op=ALU.is_equal, fill=0.0,
                                    base=0, pattern=[[-1, P]], channel_multiplier=1).then_inc(const_pool, 1)
            nc.gpsimd.memset(eps[:, :], EPS)
            nc.gpsimd.memset(minus_half[:, :], -0.5).then_inc(const_pool, 1)

            def z_times_h(X, it, l):
                pool.wait_ge(z_ready[X], at(it, L, l + 1))
                if l == 0:
                    pool.wait_ge(ht_copied[X], at(it, 1, 1))
                else:
                    pool.wait_ge(h_new[X], at(it, L, l))
                nc.gpsimd.tensor_tensor(zh[:, X, :], z_g[:, X, :], h_t[:, X, :], ALU.mult).then_inc(zh_ready[X], 1)

            with pool.Fori(0, PAIRS) as it:
                for l in range(L):
                    for X in XS:
                        z_times_h(X, it, l)

            def inverse_deviation(X, it, k):
                pool.wait_ge(mv_ready[X], at(it, 4, k + 1))
                nc.gpsimd.tensor_tensor(ve[:, X, k, :], mv[:, X, k, :, 1], eps[:, :], ALU.add).then_inc(ve_ready[X], 1)
                pool.wait_ge(ve_ready[X], at(it, 4, k + 1))
                nc.gpsimd.tensor_tensor(rstd[:, X, k, :], ve[:, X, k, :], minus_half[:, :],
                                        ALU.pow).then_inc(rstd_ready[X], 1)

            def subtract_top(X, it, u):
                pool.wait_ge(top_ready[X], at(it, U, u + 1))
                nc.gpsimd.tensor_tensor(g4(score[:, X, u % H, :]), g4(score[:, X, u % H, :]),
                                        top[:, X, u, :].unsqueeze(2).to_broadcast([P, G, P]),
                                        ALU.subtract).then_inc(sub_ready[X], 1)

            with pool.Fori(0, PAIRS) as it:
                for X in XS:
                    inverse_deviation(X, it, 0)
                for X in XS:
                    pool.wait_ge(x_normed[X], at(it, 4, 1))
                    nc.gpsimd.tensor_tensor(g4(x1b[:, X, :]), g4(x1[:, X, :]),
                                            b_row[:, :].unsqueeze(1).to_broadcast([P, G, P]),
                                            ALU.add).then_inc(x1b_ready[X], 1)
                for h in range(H):
                    for X in XS:
                        subtract_top(X, it, h)
                for k, u in ((1, UE), (2, UO)):
                    for X in XS:
                        inverse_deviation(X, it, k)
                    for X in XS:
                        subtract_top(X, it, u)
                for X in XS:
                    inverse_deviation(X, it, 3)

        @block.scalar
        def _(act):
            act.wait_ge(const_pe, 1)
            for i in range(NW):
                nc.scalar.copy(w_t[:, i, :], bank[i // 8][:, (i % 8) // 2, cols(i % 2)]).then_inc(const_act, 1)

            def split_x(X, it):
                act.wait_ge(x_loaded, at(it, 16, 16))
                act.wait_ge(tr_ready[X], at(it, L + 1, 1))
                nc.scalar.copy(h_t[:, X, :], bank[X][:, 3, :]).then_inc(ht_copied[X], 1)
                act.wait_ge(ht_copied[X], at(it, 1, 1))
                nc.scalar.copy(h_hi[:, X, :], h_t[:, X, :]).then_inc(h_hi_ready[X], 1)
                nc.scalar.copy(hn_hi[:, X, :], x_in[:, X, :]).then_inc(hn_hi_ready[X], 1)

            def split_step(X, it, l):
                if l == 0:
                    split_x(X, it)
                else:
                    act.wait_ge(tr_ready[X], at(it, L + 1, l + 1))
                    nc.scalar.copy(hn_hi[:, X, :], bank[X][:, 3, :]).then_inc(hn_hi_ready[X], 1)
                act.wait_ge(q_ready[X], at(it, L, l + 1))
                nc.scalar.copy(q_hi[:, X, :], bank[X][:, 2, :]).then_inc(q_hi_ready[X], 1)

            def gates(X, it, l):
                act.wait_ge(gates_ready[X], at(it, 3 * L, 3 * l + 1))
                nc.scalar.activation(r_g[:, X, :], bank[X][:, 0, :], ACT.Sigmoid,
                                     bias=b_gate[:, 0:1]).then_inc(r_ready[X], 1)
                act.wait_ge(gates_ready[X], at(it, 3 * L, 3 * l + 3))
                nc.scalar.activation(z_g[:, X, :], bank[X][:, 1, :], ACT.Sigmoid,
                                     bias=b_gate[:, 1:2]).then_inc(z_ready[X], 1)
                nc.scalar.activation(nz_g[:, X, :], bank[X][:, 1, :], ACT.Sigmoid,
                                     bias=nb_z[:, 0:1], scale=-1.0).then_inc(nz_ready[X], 1)
                act.wait_ge(npre_ready[X], at(it, L, l + 1))
                nc.scalar.activation(n_g[:, X, :], npre[:, X, :], ACT.Tanh,
                                     bias=b_ih_c[:, 2:3]).then_inc(n_ready[X], 1)
                if l + 1 < L:
                    act.wait_ge(h_new[X], at(it, L, l + 1))
                    nc.scalar.copy(h_hi[:, X, :], h_t[:, X, :]).then_inc(h_hi_ready[X], 1)

            act.wait_ge(const_dve, 2)
            with act.Fori(0, PAIRS) as it:
                for l in range(L):
                    split_step(0, it, l)
                    if l:
                        gates(1, it, l - 1)
                    split_step(1, it, l)
                    gates(0, it, l)
                gates(1, it, L - 1)

            act.wait_ge(const_dve, 7)

            def normalise(X, it, k, write):
                act.wait_ge(nmr_ready[X], at(it, 4, k + 1))
                for g in range(G):
                    src = y_graph(it, X, g) if k == 0 else y[:, X, cols(g)]
                    last = nc.scalar.activation(write(g), src, ACT.Identity, bias=nmr[:, X, k, g:g + 1],
                                                scale=rstd[:, X, k, g:g + 1])
                last.then_inc(x_normed[X], 1)

            def copy_xt(X, it, n, b):
                act.wait_ge(xt_ready[X], at(it, 3, n + 1))
                nc.scalar.copy(x_t[:, X, :], bank[X][:, b, :]).then_inc(xt_copied[X], 1)

            def scale_score(X, it, u, src, bias):
                act.wait_ge(u_ready[X], at(it, U, u + 1))
                nc.scalar.activation(scaled[:, X, u % 2, :], src, ACT.Identity, bias=bias,
                                     scale=SLOPE).then_inc(t_ready[X], 1)

            def exponential(X, it, u):
                act.wait_ge(sub_ready[X], at(it, U, u + 1))
                nc.scalar.activation(score[:, X, u % H, :], score[:, X, u % H, :], ACT.Exp).then_inc(p_ready[X], 1)

            def copy_pt(X, it, u, b):
                act.wait_ge(pt_ready[X], at(it, U, u + 1))
                nc.scalar.copy(prob_t[:, X, u % H, :], bank[X][:, b, :]).then_inc(pt_copied[X], 1)

            with act.Fori(0, PAIRS) as it:
                for X in XS:
                    normalise(X, it, 0, lambda g: x1[:, X, cols(g)])
                for X in XS:
                    copy_xt(X, it, 0, 0)
                for X in XS:
                    act.wait_ge(f_ready[X], at(it, 2, 1))
                    nc.scalar.copy(f1[:, X, :, :, 0:C], bank[X][:, 0, :].rearrange("p (g h c) -> p g h c", g=G, h=H)
                                   ).then_inc(f_copied[X], 1)
                for h in range(H):
                    for X in XS:
                        scale_score(X, it, h, bank[X][:, h, :], c_head_s[:, h:h + 1])
                    if h:
                        for X in XS:
                            exponential(X, it, h - 1)
                        for X in XS:
                            copy_pt(X, it, h - 1, h - 1)
                for X in XS:
                    exponential(X, it, H - 1)
                for X in XS:
                    copy_pt(X, it, H - 1, H - 1)
                for X in XS:
                    normalise(X, it, 1, lambda g: x2[:, X, g, 0:P])
                for X in XS:
                    copy_xt(X, it, 1, 0)
                    act.wait_ge(xt_copied[X], at(it, 3, 2))
                    for k in range(K):
                        last = nc.scalar.mul(xs_t[:, X, k, :], x_t[:, X, :], edge_a_c[:, k:k + 1])
                    last.then_inc(xs_ready[X], 1)
                for X in XS:
                    act.wait_ge(e_ready[X], at(it, 1, 1))
                    nc.scalar.mul(scaled[:, X, UE % 2, :], score[:, X, UE % H, :], SLOPE).then_inc(t_ready[X], 1)
                for X in XS:
                    exponential(X, it, UE)
                for X in XS:
                    copy_pt(X, it, UE, 0)
                for X in XS:
                    normalise(X, it, 2, lambda g: x3[:, X, cols(g)])
                for X in XS:
                    copy_xt(X, it, 2, 0)
                for X in XS:
                    act.wait_ge(f_ready[X], at(it, 2, 2))
                    nc.scalar.copy(f3[:, X, :, 0:P], g4(bank[X][:, 0, :])).then_inc(f_copied[X], 1)
                for X in XS:
                    scale_score(X, it, UO, bank[X][:, 1, :], 0.0)
                for X in XS:
                    exponential(X, it, UO)
                for X in XS:
                    copy_pt(X, it, UO, 1)
                act.wait_ge(out_stored, at(it, 16, 16))
                for X in XS:
                    normalise(X, it, 3, lambda g: x4[:, X, cols(g)])

        @block.vector
        def _(dve):
            V = nc.vector
            V.memset(stats[:, :, :, :, :], 0.0)
            for X in XS:
                V.memset(rden[:, X, :, :], 0.0).then_inc(y_stored[X], 1)
            V.memset(ones[:, :], 1.0).then_inc(out_stored, 16)
            V.memset(a_wide[:, :, :, :], 0.0)
            for X in XS:
                V.memset(x2[:, X, :, P:P + 1], 1.0)
                V.memset(f3[:, X, :, P:P + 1], 1.0)
                last = V.memset(f1[:, X, :, :, C:C + 1], 1.0)
            last.then_inc(const_dve, 1)
            dve.wait_ge(const_dve, 1)
            dve.wait_ge(raw_in, 16 * N_RAW)
            dve.wait_ge(const_pool, 3)
            dve_step = [0]

            def chain(ins):
                dve_step[0] += 1
                ins.then_inc(chain_sem, 1)
                dve.wait_ge(chain_sem, dve_step[0])

            chain(V.tensor_tensor(b_gate[:, :], b_ih_c[:, :], b_hh_c[:, :], ALU.add))
            chain(V.tensor_scalar(nb_z[:, :], b_gate[:, 1:2], -1.0, None, ALU.mult))
            V.tensor_copy(a_sum[:, :], a_src[:, :]).then_inc(const_dve, 1)
            dve.wait_ge(const_dve, 2)
            chain(V.tensor_tensor(a_sum[:, :], a_sum[:, :], a_dst[:, :], ALU.add))
            for h in range(H):
                rows = slice(h * C, (h + 1) * C)
                for i, col in enumerate((a_src, a_dst, a_sum)):
                    V.tensor_copy(a_wide[rows, i, h, :], col[rows, :].to_broadcast([C, P]))
            V.tensor_copy(b_wide[:, :], gat_b_c[:, :].to_broadcast([P, P]))
            for s in range(2):
                V.tensor_copy(one_wide[:, s, :], one_a_c[:, s:s + 1].to_broadcast([P, P]))
            V.tensor_scalar(b_diag[:, :], ident[:, :], gat_b_c[:, 0:1], None, ALU.mult)
            V.tensor_copy(ident_r[:, :], ident[:, :])
            V.tensor_scalar(big_ident[:, :], ident[:, :], BIG, None, ALU.mult).then_inc(const_dve, 1)
            dve.wait_ge(const_act, NW)
            for g in range(3):
                chain(V.tensor_copy(hw_hi[:, cols(g)], w_t[:, I_HH + g, :]))
                chain(V.tensor_tensor(hw_lo[:, cols(g)], w_t[:, I_HH + g, :], hw_hi[:, cols(g)].bitcast(F32), ALU.subtract))
            dve.wait_ge(const_pe, 2)
            for l in range(L):
                chain(V.tensor_copy(cw_hi[:, l, :], bank[0][:, l, 0:3 * P]))
                chain(V.tensor_tensor(cw_lo[:, l, :], bank[0][:, l, 0:3 * P], cw_hi[:, l, :].bitcast(F32), ALU.subtract))
            V.tensor_copy(v_src[:, :, :], bank[1][:, 0, :].rearrange("p (h n) -> p h n", h=H))
            V.tensor_copy(v_dst[:, :, :], bank[1][:, 1, :].rearrange("p (h n) -> p h n", h=H))
            V.tensor_copy(v_one[:, :, :], bank[1][:, 2, 0:2 * P].rearrange("p (h n) -> p h n", h=2))
            V.tensor_copy(b_row[:, :], bank[1][:, 3, 0:P])
            chain(V.tensor_copy(c_head[:, :], bank[0][:, 3, 0:H * P:P]))
            V.tensor_scalar(c_head_s[:, :], c_head[:, :], SLOPE, None, ALU.mult).then_inc(const_dve, 4)

            def split_step(X, it, l):
                if l == 0:
                    dve.wait_ge(adj_loaded, at(it, 16, 16))
                    V.tensor_scalar(edges[:, X, :], adj_in[:, X, :], 0.0, None,
                                    ALU.not_equal).then_inc(edges_ready[X], 1)
                    dve.wait_ge(h_hi_ready[X], at(it, L, 1))
                    V.tensor_tensor(h_lo[:, X, :], h_t[:, X, :], h_hi[:, X, :].bitcast(F32),
                                    ALU.subtract).then_inc(h_lo_ready[X], 1)
                    dve.wait_ge(x_loaded, at(it, 16, 16))
                    dve.wait_ge(hn_hi_ready[X], at(it, L, 1))
                    V.tensor_tensor(hn_lo[:, X, :], x_in[:, X, :], hn_hi[:, X, :].bitcast(F32),
                                    ALU.subtract).then_inc(hn_lo_ready[X], 1)
                else:
                    dve.wait_ge(hn_hi_ready[X], at(it, L, l + 1))
                    V.tensor_tensor(hn_lo[:, X, :], bank[X][:, 3, :], hn_hi[:, X, :].bitcast(F32),
                                    ALU.subtract).then_inc(hn_lo_ready[X], 1)
                dve.wait_ge(q_hi_ready[X], at(it, L, l + 1))
                V.tensor_tensor(q_lo[:, X, :], bank[X][:, 2, :], q_hi[:, X, :].bitcast(F32),
                                ALU.subtract).then_inc(q_lo_ready[X], 1)

            def update(X, it, l):
                dve.wait_ge(r_ready[X], at(it, L, l + 1))
                V.scalar_tensor_tensor(out=rn[:, X, :], in0=bank[X][:, 3, :], scalar=b_hh_c[:, 2:3],
                                       in1=r_g[:, X, :], op0=ALU.add, op1=ALU.mult).then_inc(rn_ready[X], 1)
                dve.wait_ge(rn_ready[X], at(it, L, l + 1))
                dve.wait_ge(gates_ready[X], at(it, 3 * L, 3 * l + 2))
                V.tensor_tensor(npre[:, X, :], bank[X][:, 2, :], rn[:, X, :], ALU.add).then_inc(npre_ready[X], 1)
                dve.wait_ge(n_ready[X], at(it, L, l + 1))
                dve.wait_ge(nz_ready[X], at(it, L, l + 1))
                V.tensor_tensor(nzn[:, X, :], nz_g[:, X, :], n_g[:, X, :], ALU.mult).then_inc(nzn_ready[X], 1)
                dve.wait_ge(nzn_ready[X], at(it, L, l + 1))
                dve.wait_ge(zh_ready[X], at(it, L, l + 1))
                V.tensor_tensor(h_t[:, X, :], nzn[:, X, :], zh[:, X, :], ALU.add).then_inc(h_new[X], 1)
                if l + 1 < L:
                    dve.wait_ge(h_hi_ready[X], at(it, L, l + 2))
                    V.tensor_tensor(h_lo[:, X, :], h_t[:, X, :], h_hi[:, X, :].bitcast(F32),
                                    ALU.subtract).then_inc(h_lo_ready[X], 1)

            def add_residual(X, it):
                dve.wait_ge(resid_loaded, at(it, 16, 16))
                dve.wait_ge(tr_ready[X], at(it, L + 1, L + 1))
                V.tensor_tensor(y_at(it, X), bank[X][:, 3, :], y_at(it, X), ALU.add).then_inc(y_stored[X], 1)

            with dve.Fori(0, PAIRS) as it:
                for l in range(L):
                    split_step(0, it, l)
                    if l:
                        update(1, it, l - 1)
                    split_step(1, it, l)
                    update(0, it, l)
                add_residual(0, it)
                update(1, it, L - 1)
                add_residual(1, it)

            def statistics(X, it, k):
                if k:
                    dve.wait_ge(y_ready[X], at(it, 3, k))
                for g in range(G):
                    src = y_graph(it, X, g) if k == 0 else y[:, X, cols(g)]
                    last = V.bn_stats(stats[:, X, k, g, :], src)
                last.then_inc(stats_ready[X], 1)

            def gather(it, k):
                for X in XS:
                    dve.wait_ge(stats_ready[X], at(it, 4, k + 1))
                V.memset(tick[:, :], 0.0)

            def aggregate(X, it, k):
                for g in range(G):
                    last = V.bn_aggr(mv[:, X, k, g, :], stats[:, X, k, g, :])
                last.then_inc(mv_ready[X], 1)

            def shift(X, it, k):
                dve.wait_ge(rstd_ready[X], at(it, 4, k + 1))
                V.scalar_tensor_tensor(out=nmr[:, X, k, :], in0=mv[:, X, k, :, 0], scalar=-1.0, in1=rstd[:, X, k, :],
                                       op0=ALU.mult, op1=ALU.mult).then_inc(nmr_ready[X], 1)

            def layer_norm(it, k):
                for X in XS:
                    statistics(X, it, k)
                gather(it, k)
                for X in XS:
                    aggregate(X, it, k)
                for X in XS:
                    shift(X, it, k)

            def leaky(X, it, u, src, const):
                dve.wait_ge(t_ready[X], at(it, U, u + 1))
                V.scalar_tensor_tensor(out=score[:, X, u % H, :], in0=src, scalar=const, in1=scaled[:, X, u % 2, :],
                                       op0=ALU.add, op1=ALU.max).then_inc(v_ready[X], 1)

            def maxima(X, it, u):
                dve.wait_ge(v_ready[X], at(it, U, u + 1))
                V.tensor_reduce(top[:, X, u, :], g4(score[:, X, u % H, :]), AX.X, ALU.max).then_inc(top_ready[X], 1)

            def divide(X, it, n, values, sums, inverse, result, x_res):
                dve.wait_ge(o_ready[X], at(it, 3, n + 1))
                V.reciprocal(inverse, sums).then_inc(rden_ready[X], 1)
                dve.wait_ge(rden_ready[X], at(it, 3, n + 1))
                V.tensor_tensor(result, values, inverse.unsqueeze(len(values.shape) - 1).to_broadcast(list(values.shape)),
                                ALU.mult).then_inc(o_scaled[X], 1)
                dve.wait_ge(o_scaled[X], at(it, 3, n + 1))
                V.tensor_tensor(g4(y[:, X, :]), g4(y[:, X, :]), x_res, ALU.add).then_inc(y_ready[X], 1)

            with dve.Fori(0, PAIRS) as it:
                for X in XS:
                    statistics(X, it, 0)
                gather(it, 0)
                for X in XS:
                    aggregate(X, it, 0)
                dve.wait_ge(typ_loaded, at(it, 16, 16))
                for X in XS:
                    for k in range(K):
                        V.tensor_scalar(mask[:, X, k, :], typ_in[:, X, :], float(k + 1), 1.0, ALU.is_equal, ALU.subtract)
                    V.tensor_scalar(mask[:, X, K, :], typ_in[:, X, :], 0.0, 1.0, ALU.is_gt,
                                    ALU.subtract).then_inc(masks_ready[X], 1)
                for X in XS:
                    shift(X, it, 0)
                for h in range(H):
                    for X in XS:
                        leaky(X, it, h, bank[X][:, h, :], c_head[:, h:h + 1])
                    for X in XS:
                        maxima(X, it, h)
                for X in XS:
                    dve.wait_ge(x1b_ready[X], at(it, 1, 1))
                    o = bank[X][:, :, 0:G * (C + 1)].rearrange("p h (g c) -> p h g c", g=G)
                    divide(X, it, 0, o[:, :, :, 0:C], o[:, :, :, C],
                           rden[:, X, 0, :].rearrange("p (h g) -> p h g", h=H),
                           y[:, X, :].rearrange("p (g h c) -> p h g c", g=G, h=H), g4(x1b[:, X, :]))
                layer_norm(it, 1)
                for X in XS:
                    dve.wait_ge(u_ready[X], at(it, U, UE + 1))
                    V.tensor_reduce(score[:, X, UE % H, :], bank[X][:, :, :].rearrange("p k j -> p j k"), AX.X,
                                    ALU.max).then_inc(e_ready[X], 1)
                for X in XS:
                    leaky(X, it, UE, score[:, X, UE % H, :], 0.0)
                for X in XS:
                    maxima(X, it, UE)
                for X in XS:
                    o = bank[X][:, :, 0:P + 1]
                    divide(X, it, 1, o[:, :, 0:P], o[:, :, P], rden[:, X, 1, 0:G], g4(y[:, X, :]), x2[:, X, :, 0:P])
                layer_norm(it, 2)
                for X in XS:
                    leaky(X, it, UO, bank[X][:, 1, :], 0.0)
                for X in XS:
                    maxima(X, it, UO)
                for X in XS:
                    o = bank[X][:, :, 0:P + 1]
                    divide(X, it, 2, o[:, :, 0:P], o[:, :, P], rden[:, X, 2, 0:G], g4(y[:, X, :]), g4(x3[:, X, :]))
                layer_norm(it, 3)

        @block.tensor
        def _(pe):
            mm = nc.tensor.matmul
            tr = nc.tensor.transpose

            pe.wait_ge(raw_in, 16 * N_RAW)
            pe.wait_ge(const_pool, 3)
            for i in range(NW):
                last = tr(bank[i // 8][:, (i % 8) // 2, cols(i % 2)], w_raw[:, i, :], ident[:, :])
            last.then_inc(const_pe, 1)
            pe.wait_ge(const_act, NW)
            pe.wait_ge(const_dve, 3)
            w_ih_t = w_t[:, I_IH:I_IH + 3, :].rearrange("p g o -> p (g o)")
            for l in range(L):
                mm(bank[0][:, l, 0:3 * P], w_t[:, I_W + l, :], w_ih_t, start=True, stop=True)
            for i in range(2):
                mm(bank[1][:, i, :], w_raw[:, I_GAT, :], a_wide[:, i, :, :].rearrange("p h n -> p (h n)"),
                   start=True, stop=True)
            mm(bank[1][:, 2, 0:2 * P], w_raw[:, I_ONE, :], one_wide[:, :, :].rearrange("p s n -> p (s n)"),
               start=True, stop=True)
            mm(bank[1][:, 3, 0:P], ones[:, :], b_diag[:, :], start=True, stop=True)
            mm(bank[0][:, 3, :], b_wide[:, :], a_wide[:, 2, :, :].rearrange("p h n -> p (h n)"),
               start=True, stop=True).then_inc(const_pe, 1)
            pe.wait_ge(const_dve, 7)

            def product(dst, w_hi, w_lo, m_hi, m_lo, start, stop):
                mm(dst, w_hi, m_hi, start=start, stop=False)
                mm(dst, w_lo, m_hi, start=False, stop=False)
                return mm(dst, w_hi, m_lo, start=False, stop=stop)

            def transpose_group(dst, src):
                for g in range(G):
                    last = tr(dst[:, cols(g)], src[:, cols(g)], ident[:, :])
                return last

            def first_half(X, it, l):
                R, Z, IN, HN = (bank[X][:, b, :] for b in range(4))
                if l == 0:
                    pe.wait_ge(x_loaded, at(it, 16, 16))
                    pe.wait_ge(y_stored[X], at(it, 1, 1))
                    transpose_group(HN, x_in[:, X, :]).then_inc(tr_ready[X], 1)
                else:
                    pe.wait_ge(h_new[X], at(it, L, l))
                    transpose_group(HN, h_t[:, X, :]).then_inc(tr_ready[X], 1)
                pe.wait_ge(h_lo_ready[X], at(it, L, l + 1))
                for g, dst in ((0, R), (1, Z)):
                    product(dst, hw_hi[:, cols(g)], hw_lo[:, cols(g)], h_hi[:, X, :], h_lo[:, X, :], True, False)
                pe.wait_ge(hn_lo_ready[X], at(it, L, l + 1))
                if l == 0:
                    pe.wait_ge(edges_ready[X], at(it, 1, 1))
                for g in range(G):
                    mm(IN[:, cols(g)], hn_hi[:, X, cols(g)], edges[:, X, cols(g)], start=True, stop=False)
                    last = mm(IN[:, cols(g)], hn_lo[:, X, cols(g)], edges[:, X, cols(g)], start=False, stop=True)
                last.then_inc(q_ready[X], 1)
                product(HN, hw_hi[:, cols(2)], hw_lo[:, cols(2)], h_hi[:, X, :], h_lo[:, X, :], True, True)

            def second_half(X, it, l):
                R, Z, IN, HN = (bank[X][:, b, :] for b in range(4))
                pe.wait_ge(q_lo_ready[X], at(it, L, l + 1))
                for g, dst, start in ((0, R, False), (2, IN, True), (1, Z, False)):
                    product(dst, cw_hi[:, l, cols(g)], cw_lo[:, l, cols(g)], q_hi[:, X, :], q_lo[:, X, :],
                            start, True).then_inc(gates_ready[X], 1)

            def last_transpose(X, it):
                pe.wait_ge(h_new[X], at(it, L, L))
                transpose_group(bank[X][:, 3, :], h_t[:, X, :]).then_inc(tr_ready[X], 1)

            with pe.Fori(0, PAIRS) as it:
                for l in range(L):
                    first_half(0, it, l)
                    if l:
                        second_half(1, it, l - 1)
                    first_half(1, it, l)
                    second_half(0, it, l)
                last_transpose(0, it)
                second_half(1, it, L - 1)
                last_transpose(1, it)

            def transpose_x(X, it, n, b, src):
                pe.wait_ge(x_normed[X], at(it, 4, n + 1))
                for g in range(G):
                    last = tr(bank[X][:, b, cols(g)], src(g), ident[:, :])
                last.then_inc(xt_ready[X], 1)

            def values(X, it, n, b, w):
                pe.wait_ge(xt_copied[X], at(it, 3, 1 if n == 0 else 3))
                for g in range(G):
                    last = mm(bank[X][:, b, cols(g)], x_t[:, X, cols(g)], w, start=True, stop=True)
                last.then_inc(f_ready[X], 1)

            def gat_scores(X, it, u, b, m, dst_v, src_v):
                out_b = bank[X][:, b, :]
                mm(out_b, big_ident[:, :], mask[:, X, m, :], start=True, stop=False)
                mm(out_b, dst_v, x_t[:, X, :], start=False, stop=False)
                for g in range(G):
                    last = mm(out_b[:, cols(g)], x_t[:, X, cols(g)], src_v, start=False, stop=(g == G - 1))
                last.then_inc(u_ready[X], 1)

            def transpose_p(X, it, u, b):
                pe.wait_ge(p_ready[X], at(it, U, u + 1))
                transpose_group(bank[X][:, b, :], score[:, X, u % H, :]).then_inc(pt_ready[X], 1)

            with pe.Fori(0, PAIRS) as it:
                for X in XS:
                    transpose_x(X, it, 0, 0, lambda g: x1[:, X, cols(g)])
                for X in XS:
                    values(X, it, 0, 0, w_t[:, I_GAT, :])
                for X in XS:
                    pe.wait_ge(masks_ready[X], at(it, 1, 1))
                    pe.wait_ge(f_copied[X], at(it, 2, 1))
                for h in range(H):
                    for X in XS:
                        gat_scores(X, it, h, h, 0, v_dst[:, h, :], v_src[:, h, :])
                    if h:
                        for X in XS:
                            transpose_p(X, it, h - 1, h - 1)
                for X in XS:
                    transpose_p(X, it, H - 1, H - 1)
                for X in XS:
                    for h in range(H):
                        pe.wait_ge(pt_copied[X], at(it, U, h + 1))
                        for g in range(G):
                            last = mm(bank[X][:, h, g * (C + 1):(g + 1) * (C + 1)], prob_t[:, X, h, cols(g)],
                                      f1[:, X, g, h, :], start=True, stop=True)
                    last.then_inc(o_ready[X], 1)

                for X in XS:
                    transpose_x(X, it, 1, 0, lambda g: x2[:, X, g, 0:P])
                for X in XS:
                    pe.wait_ge(xs_ready[X], at(it, 1, 1))
                    for k in range(K):
                        mm(bank[X][:, k, :], big_ident[:, :], mask[:, X, k, :], start=True, stop=False)
                        for g in range(G):
                            last = mm(bank[X][:, k, cols(g)], x_t[:, X, cols(g)], xs_t[:, X, k, cols(g)],
                                      start=False, stop=(g == G - 1))
                    last.then_inc(u_ready[X], 1)
                for X in XS:
                    transpose_p(X, it, UE, 0)
                for X in XS:
                    pe.wait_ge(pt_copied[X], at(it, U, UE + 1))
                    for g in range(G):
                        last = mm(bank[X][:, g, 0:P + 1], prob_t[:, X, UE % H, cols(g)], x2[:, X, g, :],
                                  start=True, stop=True)
                    last.then_inc(o_ready[X], 1)

                for X in XS:
                    transpose_x(X, it, 2, 0, lambda g: x3[:, X, cols(g)])
                for X in XS:
                    values(X, it, 1, 0, w_t[:, I_ONE, :])
                for X in XS:
                    gat_scores(X, it, UO, 1, K, v_one[:, 1, :], v_one[:, 0, :])
                for X in XS:
                    transpose_p(X, it, UO, 1)
                for X in XS:
                    pe.wait_ge(f_copied[X], at(it, 2, 2))
                    pe.wait_ge(pt_copied[X], at(it, U, UO + 1))
                    for g in range(G):
                        last = mm(bank[X][:, g, 0:P + 1], prob_t[:, X, UO % H, cols(g)], f3[:, X, g, :],
                                  start=True, stop=True)
                    last.then_inc(o_ready[X], 1)


_INS = ['x', 'adj', 'L0_gnn_weight', 'L0_gnn_w_ih', 'L0_gnn_w_hh', 'L0_gnn_b_ih', 'L0_gnn_b_hh', 'L1_gnn_W',
        'L1_gnn_b', 'L1_gnn_a', 'L2_gnn_a0', 'L2_gnn_a1', 'L2_gnn_a2', 'L2_gnn_a3', 'L3_gnn_W', 'L3_gnn_a']


def kernel(**inputs):
    import numpy as np
    import concourse.bacc as bacc
    from concourse.bass_utils import run_bass_kernel_spmd

    nc = bacc.Bacc("TRN2", target_bir_lowering=False, num_devices=1)
    arrays, aps = {}, {}
    for name in _INS:
        a = np.ascontiguousarray(inputs[name])
        arrays[f"in_{name}"] = a
        aps[name] = nc.dram_tensor(f"in_{name}", a.shape, mybir.dt.from_np(a.dtype), kind="ExternalInput").ap()
    out = nc.dram_tensor("out_x", inputs["x"].shape, F32, kind="ExternalOutput").ap()
    a = aps
    program(nc, a['x'], a['adj'], a['L0_gnn_weight'], a['L0_gnn_w_ih'], a['L0_gnn_w_hh'], a['L0_gnn_b_ih'],
            a['L0_gnn_b_hh'], a['L1_gnn_W'], a['L1_gnn_b'], a['L1_gnn_a'],
            [a[f'L2_gnn_a{k}'] for k in range(4)], a['L3_gnn_W'], a['L3_gnn_a'], out)
    r = run_bass_kernel_spmd(nc, [arrays], core_ids=[0])
    return r.results[0]["out_x"]
```

```python
from contextlib import ExitStack

import concourse.bass as bass
from concourse import mybir

F32 = mybir.dt.float32
F32R = mybir.dt.float32r
BF16 = mybir.dt.bfloat16
I32 = mybir.dt.int32
ALU = mybir.AluOpType
ACT = mybir.ActivationFunctionType
AX = mybir.AxisListType

P = 128
G = 4
W = G * P
EPS = 1e-5
SLOPE = 0.2
BIG = 2.0 ** 100
XS = (0, 1)
ZS = (0, 1, 2, 3)
NZ = len(ZS)


def at(it, per, k):
    return it * per + k


def at_z(it, per, k, Z):
    return it * (per * NZ) + (k * NZ + Z + 1)


def program(nc, x, adj, ggnn_w, w_ih, w_hh, b_ih, b_hh, gat_w, gat_b, gat_a, edge_a, one_w, one_a, out):
    B, N, D = x.shape
    L = ggnn_w.shape[0]
    H = gat_a.shape[0]
    C = D // H
    K = len(edge_a)
    PAIRS = B // (2 * G)
    SETS = B // (NZ * G)
    U = H + 2
    UE, UO = H, H + 1
    LOW = 32
    R = LOW + 2 * H
    assert N == P and D == P and B % (NZ * G) == 0 and K == 4 and H == 4 and L == 3

    with ExitStack() as ctx:
        def sb(name, shape, dt=F32):
            return ctx.enter_context(nc.sbuf_tensor(name, shape, dt))

        def sem(name):
            return ctx.enter_context(nc.semaphore(name))

        def sems(name):
            return [sem(f"{name}_{g}") for g in "ab"]

        ctx.enter_context(nc.allow_non_contiguous_dma(reason="small columns of biases and vectors"))

        bank = [ctx.enter_context(nc.psum_tensor(f"bank_{g}", [P, 4, W], F32)) for g in "ab"]

        def zbank(Z):
            return bank[Z // 2][:, 2 * (Z % 2):2 * (Z % 2) + 2, :]

        blocks = ([w_ih[P * i:P * i + P, :] for i in range(3)] + [w_hh[P * i:P * i + P, :] for i in range(3)]
                  + [ggnn_w[i] for i in range(L)] + [gat_w, one_w])
        I_IH, I_HH, I_W, I_GAT, I_ONE = 0, 3, 6, 6 + L, 7 + L
        NW = len(blocks)
        N_RAW = NW + 2 + 2 * H + 1 + 1 + K

        ident = sb("ident", [P, P])
        big_ident = sb("big_ident", [P, P], BF16)
        gat_w_t = sb("gat_w_t", [P, P])
        one_w_t = sb("one_w_t", [P, P])
        cw_hi = sb("cw_hi", [P, L, 3 * P], F32R)
        cw_lo = sb("cw_lo", [P, L, 3 * P], F32R)
        hw_hi = sb("hw_hi", [P, 3 * P], F32R)
        hw_lo = sb("hw_lo", [P, 3 * P], F32R)
        b_ih_c = sb("b_ih_c", [P, 3])
        b_hh_c = sb("b_hh_c", [P, 3])
        b_gate = sb("b_gate", [P, 3])
        nb_z = sb("nb_z", [P, 1])
        a_src = sb("a_src", [P, 1])
        a_dst = sb("a_dst", [P, 1])
        gat_b_c = sb("gat_b_c", [P, 1])
        one_a_c = sb("one_a_c", [P, 2])
        edge_a_c = sb("edge_a_c", [P, K])
        v_gat = sb("v_gat", [P, R])
        v_one = sb("v_one", [P, R])
        sel_1 = sb("sel_1", [R, 2 * H])
        sel = sb("sel", [R, 2 * H, P], F32R)
        c_raw = sb("c_raw", [P, 2 * H])
        c_head = sb("c_head", [P, H])
        c_head_s = sb("c_head_s", [P, H])
        b_row = sb("b_row", [P, P])
        eps = sb("eps", [P, G])
        minus_half = sb("minus_half", [P, G])
        tick = sb("tick", [P, 8])

        y_all = sb("y_all", [P, B * D])

        typ_in = sb("typ_in", [P, NZ, W], I32)
        mask = sb("mask", [P, NZ, K + 1, W], BF16)
        stats = sb("stats", [P, NZ, 4, G, 6])
        mv = sb("mv", [P, NZ, 4, G, 2])
        ve = sb("ve", [P, NZ, 4, G])
        rstd = sb("rstd", [P, NZ, 4, G])
        nmr = sb("nmr", [P, NZ, 4, G])
        top = sb("top", [P, NZ, U, G])
        rden = sb("rden", [P, NZ, 3, H * G])
        adj_in = typ_in[:, 0:2, :]

        with ExitStack() as making:
            def sb_0(name, shape, dt=F32):
                return making.enter_context(nc.sbuf_tensor(name, shape, dt))

            w_raw = sb_0("w_raw", [P, NW, P])
            w_t = sb_0("w_t", [P, NW, P])
            a_wide = sb_0("a_wide", [P, R])
            one_wide = sb_0("one_wide", [P, R])
            b_wide = sb_0("b_wide", [P, P])
            b_diag = sb_0("b_diag", [P, P])
            ones = sb_0("ones", [P, P])

        with ExitStack() as part_1:
            def sb_1(name, shape, dt=F32):
                return part_1.enter_context(nc.sbuf_tensor(name, shape, dt))

            clear = sb_1("clear", [P, 2 * NW * P + 3 * P + 2 * R])
            x_in = sb_1("x_in", [P, 2, W])
            edges = sb_1("edges", [P, 2, W], F32R)
            x_t1 = sb_1("x_t1", [P, 2, W])
            xt_hi = sb_1("xt_hi", [P, 2, W], F32R)
            xt_lo = sb_1("xt_lo", [P, 2, W], F32R)
            h_t = sb_1("h_t", [P, 2, W])
            h_hi = sb_1("h_hi", [P, 2, W], F32R)
            h_lo = sb_1("h_lo", [P, 2, W], F32R)
            hn_hi = sb_1("hn_hi", [P, 2, W], F32R)
            hn_lo = sb_1("hn_lo", [P, 2, W], F32R)
            q_hi = sb_1("q_hi", [P, 2, W], F32R)
            q_lo = sb_1("q_lo", [P, 2, W], F32R)
            r_g = sb_1("r_g", [P, 2, W])
            z_g = sb_1("z_g", [P, 2, W])
            nz_g = sb_1("nz_g", [P, 2, W])
            zh = sb_1("zh", [P, 2, W])
            rn = sb_1("rn", [P, 2, W])
            npre = sb_1("npre", [P, 2, W])
            n_g = sb_1("n_g", [P, 2, W])
            nzn = sb_1("nzn", [P, 2, W])

        x13 = sb("x13", [P, NZ, W])
        x2 = sb("x2", [P, NZ, G, P + 1])
        x_t = sb("x_t", [P, NZ, W])
        y = sb("y", [P, NZ, W])
        fv = sb("fv", [P, NZ, G * H * (C + 1)])
        rows = sb("rows", [R, NZ, W], F32R)
        scaled = sb("scaled", [P, NZ, W])
        score = sb("score", [P, NZ, H, W])
        prob_t = sb("prob_t", [P, NZ, H, W])
        x4 = score[:, :, 2, :]
        xs_t = prob_t

        def f1(Z, g, h):
            return fv[:, Z, (g * H + h) * (C + 1):(g * H + h + 1) * (C + 1)]

        def f3(Z, g):
            return fv[:, Z, g * (P + 1):(g + 1) * (P + 1)]

        raw_in = sem("raw_in")
        const_pool = sem("const_pool")
        const_dve = sem("const_dve")
        const_pe = sem("const_pe")
        const_act = sem("const_act")
        chain_sem = sem("chain_sem")

        x_loaded = sem("x_loaded")
        adj_loaded = sem("adj_loaded")
        resid_loaded = sem("resid_loaded")
        edges_ready = sems("edges_ready")
        xtr_ready = sems("xtr_ready")
        xt_hi_ready = sems("xt_hi_ready")
        xt_lo_ready = sems("xt_lo_ready")
        tr_ready = sems("tr_ready")
        h_hi_ready = sems("h_hi_ready")
        h_lo_ready = sems("h_lo_ready")
        hn_hi_ready = sems("hn_hi_ready")
        hn_lo_ready = sems("hn_lo_ready")
        q_ready = sems("q_ready")
        q_hi_ready = sems("q_hi_ready")
        q_lo_ready = sems("q_lo_ready")
        gates_ready = sems("gates_ready")
        r_ready = sems("r_ready")
        z_ready = sems("z_ready")
        nz_ready = sems("nz_ready")
        rn_ready = sems("rn_ready")
        npre_ready = sems("npre_ready")
        n_ready = sems("n_ready")
        zh_ready = sems("zh_ready")
        nzn_ready = sems("nzn_ready")
        h_new = sems("h_new")
        y_stored = sems("y_stored")

        typ_loaded = sem("typ_loaded")
        masks_ready = sem("masks_ready")
        stats_ready = sem("stats_ready")
        mv_ready = sem("mv_ready")
        ve_ready = sem("ve_ready")
        rstd_ready = sem("rstd_ready")
        nmr_ready = sem("nmr_ready")
        x_normed = sem("x_normed")
        x1b_ready = sem("x1b_ready")
        xt_ready = sem("xt_ready")
        xt_copied = sem("xt_copied")
        xs_ready = sem("xs_ready")
        f_ready = sem("f_ready")
        f_copied = sem("f_copied")
        rows_ready = sem("rows_ready")
        rows_hi_ready = sem("rows_hi_ready")
        rows_lo_ready = sem("rows_lo_ready")
        u_ready = sem("u_ready")
        e_ready = sem("e_ready")
        e_copied = sem("e_copied")
        e_joined = sem("e_joined")
        t_ready = sem("t_ready")
        v_ready = sem("v_ready")
        top_ready = sem("top_ready")
        sub_ready = sem("sub_ready")
        p_ready = sem("p_ready")
        pt_ready = sem("pt_ready")
        pt_copied = sem("pt_copied")
        o_ready = sem("o_ready")
        rden_ready = sem("rden_ready")
        o_scaled = sem("o_scaled")
        y_ready = sem("y_ready")
        out_stored = sem("out_stored")

        def g4(ap):
            return ap.rearrange("p (g n) -> p g n", g=G)

        def cols(g):
            return slice(g * P, (g + 1) * P)

        def y1_at(it, X):
            return y_all[:, bass.ds(it * (2 * W) + X * W, W)]

        def y2_graph(it, Z, g):
            return y_all[:, bass.ds(it * (NZ * W) + Z * W + g * P, P)]

        def graphs(dram, it, n):
            return dram[bass.ds(it * n, n), :, :].rearrange("b n d -> n b d")

        def tiles(tile):
            return tile.rearrange("p x (g n) -> p (x g) n", g=G)

        def slots(steps):
            return [(X, l) for l in steps for X in XS]

        def part_1_turns(engine, turn):
            turn(0, 0, 0, None, (1, 0))
            turn(1, 0, 0, (0, 0, 0), None)
            with engine.Fori(1, PAIRS) as nxt:
                it = nxt - 1
                before = (1, 0, it)
                for X, l in slots(range(1, L)):
                    turn(X, l, it, before, (0, nxt) if (X, l) == (1, L - 1) else None)
                    before = (X, l, it)
                turn(0, 0, nxt, before, (1, nxt))
                turn(1, 0, nxt, (0, 0, nxt), None)
            it = PAIRS - 1
            before = (1, 0, it)
            for X, l in slots(range(1, L)):
                turn(X, l, it, before, None)
                before = (X, l, it)
            turn(None, None, None, before, None)

        block = ctx.enter_context(nc.Block())

        @block.sync
        def _(sp):
            for i, w in enumerate(blocks):
                sp.dma_start(w_raw[:, i, :], w).then_inc(raw_in, 16)
            sp.dma_start(b_ih_c[:, :], b_ih.rearrange("(g o) -> o g", g=3)).then_inc(raw_in, 16)
            sp.dma_start(b_hh_c[:, :], b_hh.rearrange("(g o) -> o g", g=3)).then_inc(raw_in, 16)
            for h in range(H):
                head = slice(h * C, (h + 1) * C)
                sp.dma_start(a_src[head, :], gat_a[h, 0:C].rearrange("(c o) -> c o", o=1)).then_inc(raw_in, 16)
                sp.dma_start(a_dst[head, :], gat_a[h, C:2 * C].rearrange("(c o) -> c o", o=1)).then_inc(raw_in, 16)
            sp.dma_start(gat_b_c[:, :], gat_b.rearrange("(c o) -> c o", o=1)).then_inc(raw_in, 16)
            sp.dma_start(one_a_c[:, :], one_a.rearrange("a (s c) -> c (a s)", s=2)).then_inc(raw_in, 16)
            for k in range(K):
                sp.dma_start(edge_a_c[:, k:k + 1], edge_a[k].rearrange("(c o) -> c o", o=1)).then_inc(raw_in, 16)

            def load_pair(it):
                sp.dma_start(tiles(x_in[:, :, :]), graphs(x, it, 2 * G)).then_inc(x_loaded, 16)
                sp.dma_start(tiles(adj_in), graphs(adj, it, 2 * G)).then_inc(adj_loaded, 16)
                sp.dma_start(y_all[:, bass.ds(it * (2 * W), 2 * W)].rearrange("p (b d) -> p b d", d=D),
                             graphs(x, it, 2 * G)).then_inc(resid_loaded, 16)

            load_pair(0)
            with sp.Fori(1, PAIRS) as it:
                for X in XS:
                    sp.wait_ge(xtr_ready[X], it)
                    sp.wait_ge(hn_lo_ready[X], at(it - 1, L, 1))
                    sp.wait_ge(edges_ready[X], it)
                sp.wait_ge(resid_loaded, at(it - 1, 16, 16))
                load_pair(it)

            for X in XS:
                sp.wait_ge(edges_ready[X], PAIRS)

            def load_types(it):
                for half in range(2):
                    sp.dma_start(tiles(typ_in[:, 2 * half:2 * half + 2, :]),
                                 adj[bass.ds(it * (NZ * G) + half * (2 * G), 2 * G), :, :].rearrange("b n d -> n b d")
                                 ).then_inc(typ_loaded, 16)

            load_types(0)

            def store_group(it, Z):
                sp.dma_start(out[bass.ds(it * (NZ * G) + Z * G, G), :, :].rearrange("b n d -> n b d"),
                             g4(x4[:, Z, :])).then_inc(out_stored, 16)

            with sp.Fori(1, SETS) as it:
                sp.wait_ge(masks_ready, at(it - 1, NZ, NZ))
                load_types(it)
                for Z in ZS:
                    sp.wait_ge(x_normed, at_z(it - 1, 4, 3, Z))
                    store_group(it - 1, Z)
            for Z in ZS:
                sp.wait_ge(x_normed, at_z(SETS - 1, 4, 3, Z))
                store_group(SETS - 1, Z)
            sp.wait_ge(out_stored, 16 * NZ * (SETS + 1))

        @block.gpsimd
        def _(pool):
            nc.gpsimd.memset(ident[:, :], 1.0).then_inc(const_pool, 1)
            pool.wait_ge(const_pool, 1)
            nc.gpsimd.affine_select(out=ident[:, :], in_=ident[:, :], compare_op=ALU.is_equal, fill=0.0,
                                    base=0, pattern=[[-1, P]], channel_multiplier=1).then_inc(const_pool, 1)
            nc.gpsimd.memset(eps[:, :], EPS)
            nc.gpsimd.memset(minus_half[:, :], -0.5).then_inc(const_pool, 1)

            with pool.Fori(0, PAIRS) as it:
                for X, l in slots(range(L)):
                    pool.wait_ge(z_ready[X], at(it, L, l + 1))
                    if l == 0:
                        pool.wait_ge(xt_hi_ready[X], at(it, 1, 1))
                    else:
                        pool.wait_ge(h_new[X], at(it, L, l))
                    old = x_t1 if l == 0 else h_t
                    nc.gpsimd.tensor_tensor(zh[:, X, :], z_g[:, X, :], old[:, X, :],
                                            ALU.mult).then_inc(zh_ready[X], 1)

            def inverse_deviation(it, k):
                for Z in ZS:
                    pool.wait_ge(mv_ready, at_z(it, 4, k, Z))
                    nc.gpsimd.tensor_tensor(ve[:, Z, k, :], mv[:, Z, k, :, 1], eps[:, :], ALU.add).then_inc(ve_ready, 1)
                    pool.wait_ge(ve_ready, at_z(it, 4, k, Z))
                    nc.gpsimd.tensor_tensor(rstd[:, Z, k, :], ve[:, Z, k, :], minus_half[:, :],
                                            ALU.pow).then_inc(rstd_ready, 1)

            def subtract_top(it, u):
                for Z in ZS:
                    s = g4(score[:, Z, u % H, :])
                    pool.wait_ge(top_ready, at_z(it, U, u, Z))
                    nc.gpsimd.tensor_tensor(s, s, top[:, Z, u, :].unsqueeze(2).to_broadcast([P, G, P]),
                                            ALU.subtract).then_inc(sub_ready, 1)

            def add_residual(it, n, res):
                for Z in ZS:
                    pool.wait_ge(o_scaled, at_z(it, 3, n, Z))
                    nc.gpsimd.tensor_tensor(g4(y[:, Z, :]), g4(scaled[:, Z, :]), res(Z), ALU.add).then_inc(y_ready, 1)

            with pool.Fori(0, SETS) as it:
                inverse_deviation(it, 0)
                for Z in ZS:
                    pool.wait_ge(x_normed, at_z(it, 4, 0, Z))
                    nc.gpsimd.tensor_tensor(g4(y[:, Z, :]), g4(x13[:, Z, :]),
                                            b_row[:, :].unsqueeze(1).to_broadcast([P, G, P]),
                                            ALU.add).then_inc(x1b_ready, 1)
                for h in range(H):
                    subtract_top(it, h)
                pool.wait_ge(x1b_ready, at_z(it, 1, 0, NZ - 1))
                add_residual(it, 0, lambda Z: g4(y[:, Z, :]))
                inverse_deviation(it, 1)
                subtract_top(it, UE)
                add_residual(it, 1, lambda Z: x2[:, Z, :, 0:P])
                inverse_deviation(it, 2)
                subtract_top(it, UO)
                add_residual(it, 2, lambda Z: g4(x13[:, Z, :]))
                inverse_deviation(it, 3)

        @block.scalar
        def _(act):
            act.wait_ge(const_pe, 1)
            for i in range(NW):
                dst = {I_GAT: gat_w_t, I_ONE: one_w_t}.get(i)
                nc.scalar.copy(w_t[:, i, :] if dst is None else dst[:, :],
                               bank[i // 8][:, (i % 8) // 2, cols(i % 2)]).then_inc(const_act, 1)

            def copy_x_t(X, it):
                act.wait_ge(xtr_ready[X], at(it, 1, 1))
                nc.scalar.copy(x_t1[:, X, :], bank[X][:, 3, :])
                nc.scalar.copy(xt_hi[:, X, :], bank[X][:, 3, :]).then_inc(xt_hi_ready[X], 1)

            def turn(X, l, it, before, x_next):
                if before:
                    Y, m, jt = before
                    act.wait_ge(gates_ready[Y], at(jt, 3 * L, 3 * m + 1))
                    nc.scalar.activation(r_g[:, Y, :], bank[Y][:, 0, :], ACT.Sigmoid,
                                         bias=b_gate[:, 0:1]).then_inc(r_ready[Y], 1)
                    act.wait_ge(gates_ready[Y], at(jt, 3 * L, 3 * m + 3))
                    nc.scalar.activation(z_g[:, Y, :], bank[Y][:, 1, :], ACT.Sigmoid,
                                         bias=b_gate[:, 1:2]).then_inc(z_ready[Y], 1)
                if X is not None:
                    if l == 0:
                        act.wait_ge(x_loaded, at(it, 16, 16))
                        nc.scalar.copy(hn_hi[:, X, :], x_in[:, X, :]).then_inc(hn_hi_ready[X], 1)
                    else:
                        act.wait_ge(tr_ready[X], at(it, L, l))
                        nc.scalar.copy(hn_hi[:, X, :], bank[X][:, 3, :]).then_inc(hn_hi_ready[X], 1)
                if before:
                    act.wait_ge(npre_ready[Y], at(jt, L, m + 1))
                    nc.scalar.activation(n_g[:, Y, :], npre[:, Y, :], ACT.Tanh,
                                         bias=b_ih_c[:, 2:3]).then_inc(n_ready[Y], 1)
                    nc.scalar.activation(nz_g[:, Y, :], bank[Y][:, 1, :], ACT.Sigmoid,
                                         bias=nb_z[:, 0:1], scale=-1.0).then_inc(nz_ready[Y], 1)
                if X is not None:
                    act.wait_ge(q_ready[X], at(it, L, l + 1))
                    nc.scalar.copy(q_hi[:, X, :], bank[X][:, 2, :]).then_inc(q_hi_ready[X], 1)
                if before and m + 1 < L:
                    act.wait_ge(h_new[Y], at(jt, L, m + 1))
                    nc.scalar.copy(h_hi[:, Y, :], h_t[:, Y, :]).then_inc(h_hi_ready[Y], 1)
                if x_next:
                    copy_x_t(*x_next)

            act.wait_ge(const_dve, 2)
            copy_x_t(0, 0)
            part_1_turns(act, turn)

            act.wait_ge(const_dve, 7)

            def normalise(it, k, write):
                for Z in ZS:
                    act.wait_ge(nmr_ready, at_z(it, 4, k, Z))
                    if k == 0:
                        nc.scalar.copy(tick[:, Z:Z + 1], minus_half[:, 0:1])
                    for g in range(G):
                        src = y2_graph(it, Z, g) if k == 0 else y[:, Z, cols(g)]
                        last = nc.scalar.activation(write(Z, g), src, ACT.Identity, bias=nmr[:, Z, k, g:g + 1],
                                                    scale=rstd[:, Z, k, g:g + 1])
                    last.then_inc(x_normed, 1)

            def copy_xt(it, n):
                for Z in ZS:
                    act.wait_ge(xt_ready, at_z(it, 3, n, Z))
                    nc.scalar.copy(x_t[:, Z, :], zbank(Z)[:, 0, :]).then_inc(xt_copied, 1)

            def high_rows(it, n):
                for Z in ZS:
                    act.wait_ge(rows_ready, at_z(it, 2, n, Z))
                    nc.scalar.copy(rows[:, Z, :], zbank(Z)[0:R, 1, :]).then_inc(rows_hi_ready, 1)

            def scale_score(it, u, n, src, bias):
                for Z in ZS:
                    if n is not None:
                        act.wait_ge(u_ready, at_z(it, H + 1, n, Z))
                    else:
                        act.wait_ge(e_joined, at_z(it, K - 1, K - 2, Z))
                    if u:
                        act.wait_ge(v_ready, at_z(it, U, u - 1, Z))
                    nc.scalar.activation(scaled[:, Z, :], src(Z), ACT.Identity, bias=bias,
                                         scale=SLOPE).then_inc(t_ready, 1)

            def exponential(it, u):
                for Z in ZS:
                    act.wait_ge(sub_ready, at_z(it, U, u, Z))
                    nc.scalar.activation(score[:, Z, u % H, :], score[:, Z, u % H, :], ACT.Exp).then_inc(p_ready, 1)

            def copy_pt(it, u, b):
                for Z in ZS:
                    act.wait_ge(pt_ready, at_z(it, U, u, Z))
                    nc.scalar.copy(prob_t[:, Z, u % H, :], zbank(Z)[:, b, :]).then_inc(pt_copied, 1)

            with act.Fori(0, SETS) as it:
                normalise(it, 0, lambda Z, g: x13[:, Z, cols(g)])
                copy_xt(it, 0)
                for Z in ZS:
                    act.wait_ge(f_ready, at_z(it, 2, 0, Z))
                    nc.scalar.copy(fv[:, Z, :].rearrange("p (h c) -> p h c", c=C + 1)[:, :, 0:C],
                                   zbank(Z)[:, 0, :].rearrange("p (h c) -> p h c", c=C)).then_inc(f_copied, 1)
                high_rows(it, 0)
                for h in range(H):
                    scale_score(it, h, h, lambda Z: zbank(Z)[:, h % 2, :], c_head_s[:, h:h + 1])
                    if h:
                        exponential(it, h - 1)
                        copy_pt(it, h - 1, (h - 1) % 2)
                exponential(it, H - 1)
                copy_pt(it, H - 1, (H - 1) % 2)

                normalise(it, 1, lambda Z, g: x2[:, Z, g, 0:P])
                for Z in ZS:
                    act.wait_ge(xt_ready, at_z(it, 3, 1, Z))
                    nc.scalar.copy(x_t[:, Z, :], zbank(Z)[:, 0, :]).then_inc(xt_copied, 1)
                    act.wait_ge(xt_copied, at_z(it, 3, 1, Z))
                    for k in range(K):
                        last = nc.scalar.mul(xs_t[:, Z, k, :], x_t[:, Z, :], edge_a_c[:, k:k + 1])
                    last.then_inc(xs_ready, 1)
                for Z in ZS:
                    act.wait_ge(e_ready, at_z(it, K, 0, Z))
                    nc.scalar.copy(score[:, Z, UE % H, :], zbank(Z)[:, 0, :]).then_inc(e_copied, 1)
                scale_score(it, UE, None, lambda Z: score[:, Z, UE % H, :], 0.0)
                exponential(it, UE)
                copy_pt(it, UE, 0)

                normalise(it, 2, lambda Z, g: x13[:, Z, cols(g)])
                copy_xt(it, 2)
                for Z in ZS:
                    act.wait_ge(f_ready, at_z(it, 2, 1, Z))
                    nc.scalar.copy(fv[:, Z, 0:G * (P + 1)].rearrange("p (g n) -> p g n", g=G)[:, :, 0:P],
                                   g4(zbank(Z)[:, 0, :])).then_inc(f_copied, 1)
                high_rows(it, 1)
                scale_score(it, UO, H, lambda Z: zbank(Z)[:, 0, :], 0.0)
                exponential(it, UO)
                copy_pt(it, UO, 0)
                normalise(it, 3, lambda Z, g: x4[:, Z, cols(g)])

        @block.vector
        def _(dve):
            V = nc.vector
            V.memset(ones[:, :], 1.0).then_inc(out_stored, 16 * NZ)
            V.memset(one_wide[:, :], 0.0)
            V.memset(a_wide[:, :], 0.0).then_inc(const_dve, 1)
            dve.wait_ge(const_dve, 1)
            dve.wait_ge(raw_in, 16 * N_RAW)
            dve.wait_ge(const_pool, 3)
            dve_step = [0]

            def chain(ins):
                dve_step[0] += 1
                ins.then_inc(chain_sem, 1)
                dve.wait_ge(chain_sem, dve_step[0])

            chain(V.tensor_tensor(b_gate[:, :], b_ih_c[:, :], b_hh_c[:, :], ALU.add))
            V.tensor_scalar(nb_z[:, :], b_gate[:, 1:2], -1.0, None, ALU.mult).then_inc(const_dve, 1)
            for twice in (0, LOW):
                for h in range(H):
                    head = slice(h * C, (h + 1) * C)
                    V.tensor_copy(a_wide[head, twice + h:twice + h + 1], a_src[head, :])
                    V.tensor_copy(a_wide[head, twice + H + h:twice + H + h + 1], a_dst[head, :])
                V.tensor_copy(one_wide[:, twice:twice + 2], one_a_c[:, :])
            V.tensor_copy(b_wide[:, :], gat_b_c[:, :].to_broadcast([P, P]))
            V.tensor_scalar(b_diag[:, :], ident[:, :], gat_b_c[:, 0:1], None, ALU.mult)
            chain(V.tensor_tensor(sel_1[:, :], ident[0:R, 0:2 * H], ident[0:R, LOW:R], ALU.add))
            for r in range(2 * H):
                V.tensor_copy(sel[:, r, :], sel_1[:, r:r + 1].to_broadcast([R, P]))
            V.tensor_scalar(big_ident[:, :], ident[:, :], BIG, None, ALU.mult).then_inc(const_dve, 1)
            dve.wait_ge(const_act, NW)
            for g in range(3):
                chain(V.tensor_copy(hw_hi[:, cols(g)], w_t[:, I_HH + g, :]))
                chain(V.tensor_tensor(hw_lo[:, cols(g)], w_t[:, I_HH + g, :], hw_hi[:, cols(g)].bitcast(F32), ALU.subtract))
            dve.wait_ge(const_pe, 2)
            for l in range(L):
                chain(V.tensor_copy(cw_hi[:, l, :], bank[0][:, l, 0:3 * P]))
                chain(V.tensor_tensor(cw_lo[:, l, :], bank[0][:, l, 0:3 * P], cw_hi[:, l, :].bitcast(F32), ALU.subtract))
            V.tensor_copy(v_gat[:, :], bank[1][:, 0, 0:R])
            V.tensor_copy(v_one[:, :], bank[1][:, 1, 0:R])
            V.tensor_copy(b_row[:, :], bank[1][:, 3, 0:P])
            chain(V.tensor_copy(c_raw[:, :], bank[1][:, 2, 0:2 * H]))
            chain(V.tensor_tensor(c_head[:, :], c_raw[:, 0:H], c_raw[:, H:2 * H], ALU.add))
            V.tensor_scalar(c_head_s[:, :], c_head[:, :], SLOPE, None, ALU.mult).then_inc(const_dve, 4)

            def low_x_t(X, it):
                dve.wait_ge(xt_hi_ready[X], at(it, 1, 1))
                V.tensor_tensor(xt_lo[:, X, :], x_t1[:, X, :], xt_hi[:, X, :].bitcast(F32),
                                ALU.subtract).then_inc(xt_lo_ready[X], 1)

            def store_y(X, it):
                dve.wait_ge(resid_loaded, at(it, 16, 16))
                dve.wait_ge(tr_ready[X], at(it, L, L))
                V.tensor_tensor(y1_at(it, X), bank[X][:, 2, :], y1_at(it, X), ALU.add).then_inc(y_stored[X], 1)

            def turn(X, l, it, before, x_next):
                if before:
                    Y, m, jt = before
                    dve.wait_ge(r_ready[Y], at(jt, L, m + 1))
                    V.scalar_tensor_tensor(out=rn[:, Y, :], in0=bank[Y][:, 3, :], scalar=b_hh_c[:, 2:3],
                                           in1=r_g[:, Y, :], op0=ALU.add, op1=ALU.mult).then_inc(rn_ready[Y], 1)
                    dve.wait_ge(rn_ready[Y], at(jt, L, m + 1))
                    dve.wait_ge(gates_ready[Y], at(jt, 3 * L, 3 * m + 2))
                    V.tensor_tensor(npre[:, Y, :], bank[Y][:, 2, :], rn[:, Y, :], ALU.add).then_inc(npre_ready[Y], 1)
                if X is not None:
                    if l == 0:
                        dve.wait_ge(adj_loaded, at(it, 16, 16))
                        V.tensor_scalar(edges[:, X, :], adj_in[:, X, :], 0.0, None,
                                        ALU.not_equal).then_inc(edges_ready[X], 1)
                        dve.wait_ge(x_loaded, at(it, 16, 16))
                    dve.wait_ge(hn_hi_ready[X], at(it, L, l + 1))
                    src = x_in[:, X, :] if l == 0 else bank[X][:, 3, :]
                    V.tensor_tensor(hn_lo[:, X, :], src, hn_hi[:, X, :].bitcast(F32),
                                    ALU.subtract).then_inc(hn_lo_ready[X], 1)
                    if l == 0 and not isinstance(it, int):
                        store_y(X, it - 1)
                if before:
                    dve.wait_ge(nz_ready[Y], at(jt, L, m + 1))
                    V.tensor_tensor(nzn[:, Y, :], nz_g[:, Y, :], n_g[:, Y, :], ALU.mult).then_inc(nzn_ready[Y], 1)
                if X is not None:
                    dve.wait_ge(q_hi_ready[X], at(it, L, l + 1))
                    V.tensor_tensor(q_lo[:, X, :], bank[X][:, 2, :], q_hi[:, X, :].bitcast(F32),
                                    ALU.subtract).then_inc(q_lo_ready[X], 1)
                if before:
                    dve.wait_ge(nzn_ready[Y], at(jt, L, m + 1))
                    dve.wait_ge(zh_ready[Y], at(jt, L, m + 1))
                    V.tensor_tensor(h_t[:, Y, :], nzn[:, Y, :], zh[:, Y, :], ALU.add).then_inc(h_new[Y], 1)
                    if m + 1 < L:
                        dve.wait_ge(h_hi_ready[Y], at(jt, L - 1, m + 1))
                        V.tensor_tensor(h_lo[:, Y, :], h_t[:, Y, :], h_hi[:, Y, :].bitcast(F32),
                                        ALU.subtract).then_inc(h_lo_ready[Y], 1)
                if x_next:
                    low_x_t(*x_next)

            low_x_t(0, 0)
            part_1_turns(dve, turn)
            for X in XS:
                store_y(X, PAIRS - 1)

            for Z in ZS:
                V.memset(x2[:, Z, :, P:P + 1], 1.0)

            def statistics(it, k):
                for Z in ZS:
                    if k:
                        dve.wait_ge(y_ready, at_z(it, 3, k - 1, Z))
                    for g in range(G):
                        src = y2_graph(it, Z, g) if k == 0 else y[:, Z, cols(g)]
                        last = V.bn_stats(stats[:, Z, k, g, :], src)
                    last.then_inc(stats_ready, 1)

            def aggregate(it, k):
                dve.wait_ge(stats_ready, at_z(it, 4, k, NZ - 1))
                V.memset(tick[:, 4:5], 0.0)
                for Z in ZS:
                    for g in range(G):
                        last = V.bn_aggr(mv[:, Z, k, g, :], stats[:, Z, k, g, :])
                    last.then_inc(mv_ready, 1)

            def shift(it, k):
                for Z in ZS:
                    dve.wait_ge(rstd_ready, at_z(it, 4, k, Z))
                    V.scalar_tensor_tensor(out=nmr[:, Z, k, :], in0=mv[:, Z, k, :, 0], scalar=-1.0, in1=rstd[:, Z, k, :],
                                           op0=ALU.mult, op1=ALU.mult).then_inc(nmr_ready, 1)

            def low_rows(it, n):
                for Z in ZS:
                    dve.wait_ge(rows_hi_ready, at_z(it, 2, n, Z))
                    V.tensor_tensor(rows[LOW:R, Z, :], zbank(Z)[LOW:R, 1, :], rows[LOW:R, Z, :].bitcast(F32),
                                    ALU.subtract).then_inc(rows_lo_ready, 1)

            def leaky(it, u, src, const):
                for Z in ZS:
                    dve.wait_ge(t_ready, at_z(it, U, u, Z))
                    V.scalar_tensor_tensor(out=score[:, Z, u % H, :], in0=src(Z), scalar=const, in1=scaled[:, Z, :],
                                           op0=ALU.add, op1=ALU.max).then_inc(v_ready, 1)

            def maxima(it, u):
                for Z in ZS:
                    dve.wait_ge(v_ready, at_z(it, U, u, Z))
                    V.tensor_reduce(top[:, Z, u, :], g4(score[:, Z, u % H, :]), AX.X, ALU.max).then_inc(top_ready, 1)

            def divide(it, n, heads):
                c = D // heads
                for Z in ZS:
                    o = zbank(Z)[:, :, 0:2 * heads * (c + 1)].rearrange("p b (m c) -> p b m c", c=c + 1)
                    inverse = rden[:, Z, n, 0:G * heads].rearrange("p (b m) -> p b m", b=2)
                    dve.wait_ge(o_ready, at_z(it, 3, n, Z))
                    V.reciprocal(inverse, o[:, :, :, c]).then_inc(rden_ready, 1)
                    dve.wait_ge(rden_ready, at_z(it, 3, n, Z))
                    V.tensor_tensor(scaled[:, Z, :].rearrange("p (b m c) -> p b m c", b=2, c=c), o[:, :, :, 0:c],
                                    inverse.unsqueeze(3).to_broadcast([P, 2, 2 * heads, c]),
                                    ALU.mult).then_inc(o_scaled, 1)

            with dve.Fori(0, SETS) as it:
                statistics(it, 0)
                aggregate(it, 0)
                dve.wait_ge(typ_loaded, at(it, 32, 32))
                for Z in ZS:
                    for k in range(K):
                        V.tensor_scalar(mask[:, Z, k, :], typ_in[:, Z, :], float(k + 1), 1.0, ALU.is_equal, ALU.subtract)
                    V.tensor_scalar(mask[:, Z, K, :], typ_in[:, Z, :], 0.0, 1.0, ALU.is_gt,
                                    ALU.subtract).then_inc(masks_ready, 1)
                    if Z == 0:
                        shift(it, 0)
                for Z in ZS:
                    V.memset(fv[:, Z, :].rearrange("p (h c) -> p h c", c=C + 1)[:, :, C:C + 1], 1.0)
                low_rows(it, 0)
                for h in range(H):
                    if h == 2:
                        dve.wait_ge(out_stored, at(it, 16 * NZ, 16 * NZ))
                    leaky(it, h, lambda Z: zbank(Z)[:, h % 2, :], c_head[:, h:h + 1])
                    maxima(it, h)
                divide(it, 0, H)
                statistics(it, 1)
                aggregate(it, 1)
                shift(it, 1)
                for k in range(1, K):
                    for Z in ZS:
                        dve.wait_ge(e_ready, at_z(it, K, k, Z))
                        if k == 1:
                            dve.wait_ge(e_copied, at_z(it, 1, 0, Z))
                        else:
                            dve.wait_ge(e_joined, at_z(it, K - 1, k - 2, Z))
                        V.tensor_tensor(score[:, Z, UE % H, :], zbank(Z)[:, k % 2, :], score[:, Z, UE % H, :],
                                        ALU.max).then_inc(e_joined, 1)
                leaky(it, UE, lambda Z: score[:, Z, UE % H, :], 0.0)
                maxima(it, UE)
                divide(it, 1, 1)
                for Z in ZS:
                    V.memset(fv[:, Z, 0:G * (P + 1)].rearrange("p (g n) -> p g n", g=G)[:, :, P:P + 1], 1.0)
                statistics(it, 2)
                aggregate(it, 2)
                shift(it, 2)
                low_rows(it, 1)
                leaky(it, UO, lambda Z: zbank(Z)[:, 0, :], 0.0)
                maxima(it, UO)
                divide(it, 2, 1)
                statistics(it, 3)
                aggregate(it, 3)
                shift(it, 3)

        @block.tensor
        def _(pe):
            mm = nc.tensor.matmul
            tr = nc.tensor.transpose

            pe.wait_ge(raw_in, 16 * N_RAW)
            pe.wait_ge(const_pool, 3)
            for i in range(NW):
                last = tr(bank[i // 8][:, (i % 8) // 2, cols(i % 2)], w_raw[:, i, :], ident[:, :])
            last.then_inc(const_pe, 1)
            pe.wait_ge(const_act, NW)
            pe.wait_ge(const_dve, 3)
            w_ih_t = w_t[:, I_IH:I_IH + 3, :].rearrange("p g o -> p (g o)")
            for l in range(L):
                mm(bank[0][:, l, 0:3 * P], w_t[:, I_W + l, :], w_ih_t, start=True, stop=True)
            mm(bank[1][:, 0, 0:R], w_raw[:, I_GAT, :], a_wide[:, :], start=True, stop=True)
            mm(bank[1][:, 1, 0:R], w_raw[:, I_ONE, :], one_wide[:, :], start=True, stop=True)
            mm(bank[1][:, 2, 0:R], b_wide[:, :], a_wide[:, :], start=True, stop=True)
            mm(bank[1][:, 3, 0:P], ones[:, :], b_diag[:, :], start=True, stop=True).then_inc(const_pe, 1)
            pe.wait_ge(const_dve, 7)

            def product(dst, w_hi, w_lo, m_hi, m_lo, start, stop):
                mm(dst, w_hi, m_hi, start=start, stop=False)
                mm(dst, w_lo, m_hi, start=False, stop=False)
                return mm(dst, w_hi, m_lo, start=False, stop=stop)

            def transpose_group(dst, src):
                for g in range(G):
                    last = tr(dst[:, cols(g)], src[:, cols(g)], ident[:, :])
                return last

            def transpose_result(X, it):
                pe.wait_ge(h_new[X], at(it, L, L))
                transpose_group(bank[X][:, 2, :], h_t[:, X, :]).then_inc(tr_ready[X], 1)

            def transpose_input(X, it, first):
                pe.wait_ge(x_loaded, at(it, 16, 16))
                if not first:
                    pe.wait_ge(rn_ready[X], at(it - 1, L, L))
                transpose_group(bank[X][:, 3, :], x_in[:, X, :]).then_inc(xtr_ready[X], 1)

            def turn(X, l, it, before, x_next):
                if X is None:
                    return
                RB, ZB, IN, HN = (bank[X][:, b, :] for b in range(4))
                next_pair = l == 0 and not isinstance(it, int)
                if l == 0:
                    if next_pair:
                        transpose_result(X, it - 1)
                    pe.wait_ge(xt_lo_ready[X], at(it, 1, 1))
                    hh, hl = xt_hi, xt_lo
                else:
                    pe.wait_ge(h_new[X], at(it, L, l))
                    transpose_group(HN, h_t[:, X, :]).then_inc(tr_ready[X], 1)
                    pe.wait_ge(h_lo_ready[X], at(it, L - 1, l))
                    hh, hl = h_hi, h_lo
                for g, dst in ((0, RB), (1, ZB)):
                    product(dst, hw_hi[:, cols(g)], hw_lo[:, cols(g)], hh[:, X, :], hl[:, X, :], True, False)
                pe.wait_ge(hn_lo_ready[X], at(it, L, l + 1))
                if l == 0:
                    pe.wait_ge(edges_ready[X], at(it, 1, 1))
                    if next_pair:
                        pe.wait_ge(y_stored[X], at(it - 1, 1, 1))
                for g in range(G):
                    mm(IN[:, cols(g)], hn_hi[:, X, cols(g)], edges[:, X, cols(g)], start=True, stop=False)
                    last = mm(IN[:, cols(g)], hn_lo[:, X, cols(g)], edges[:, X, cols(g)], start=False, stop=True)
                last.then_inc(q_ready[X], 1)
                product(HN, hw_hi[:, cols(2)], hw_lo[:, cols(2)], hh[:, X, :], hl[:, X, :], True, True)
                if x_next:
                    transpose_input(*x_next, first=isinstance(x_next[1], int))
                pe.wait_ge(q_lo_ready[X], at(it, L, l + 1))
                for g, dst, start in ((0, RB, False), (2, IN, True), (1, ZB, False)):
                    product(dst, cw_hi[:, l, cols(g)], cw_lo[:, l, cols(g)], q_hi[:, X, :], q_lo[:, X, :],
                            start, True).then_inc(gates_ready[X], 1)

            transpose_input(0, 0, first=True)
            part_1_turns(pe, turn)
            for X in XS:
                transpose_result(X, PAIRS - 1)

            def transpose_x(it, n, src):
                for Z in ZS:
                    pe.wait_ge(x_normed, at_z(it, 4, n, Z))
                    for g in range(G):
                        last = tr(zbank(Z)[:, 0, cols(g)], src(Z, g), ident[:, :])
                    last.then_inc(xt_ready, 1)

            def values_and_rows(it, n, w, v):
                for Z in ZS:
                    pe.wait_ge(xt_copied, at_z(it, 3, 2 * n, Z))
                    for g in range(G):
                        last = mm(zbank(Z)[:, 0, cols(g)], x_t[:, Z, cols(g)], w, start=True, stop=True)
                    last.then_inc(f_ready, 1)
                    mm(zbank(Z)[0:R, 1, :], v, x_t[:, Z, :], start=True, stop=True).then_inc(rows_ready, 1)

            def gat_scores(it, Z, b, m, src, dst):
                out_b = zbank(Z)[:, b, :]
                mm(out_b, big_ident[:, :], mask[:, Z, m, :], start=True, stop=False)
                mm(out_b, sel[:, dst, :], rows[:, Z, :], start=False, stop=False)
                for g in range(G):
                    last = mm(out_b[:, cols(g)], rows[:, Z, cols(g)], sel[:, src, :], start=False, stop=(g == G - 1))
                last.then_inc(u_ready, 1)

            def transpose_p(it, u, b):
                for Z in ZS:
                    pe.wait_ge(p_ready, at_z(it, U, u, Z))
                    transpose_group(zbank(Z)[:, b, :], score[:, Z, u % H, :]).then_inc(pt_ready, 1)

            with pe.Fori(0, SETS) as it:
                transpose_x(it, 0, lambda Z, g: x13[:, Z, cols(g)])
                values_and_rows(it, 0, gat_w_t[:, :], v_gat[:, :])
                for h in range(H):
                    for Z in ZS:
                        if h == 0:
                            pe.wait_ge(masks_ready, at_z(it, 1, 0, Z))
                            pe.wait_ge(f_copied, at_z(it, 2, 0, Z))
                            pe.wait_ge(rows_lo_ready, at_z(it, 2, 0, Z))
                        elif h > 1:
                            pe.wait_ge(pt_copied, at_z(it, U, h - 2, Z))
                        gat_scores(it, Z, h % 2, 0, h, H + h)
                    if h:
                        transpose_p(it, h - 1, (h - 1) % 2)
                transpose_p(it, H - 1, (H - 1) % 2)
                for Z in ZS:
                    pe.wait_ge(pt_copied, at_z(it, U, H - 1, Z))
                    for g in range(G):
                        for h in range(H):
                            m = ((g % 2) * H + h) * (C + 1)
                            last = mm(zbank(Z)[:, g // 2, m:m + C + 1], prob_t[:, Z, h, cols(g)], f1(Z, g, h),
                                      start=True, stop=True)
                    last.then_inc(o_ready, 1)

                transpose_x(it, 1, lambda Z, g: x2[:, Z, g, 0:P])
                for k in range(K):
                    for Z in ZS:
                        if k == 0:
                            pe.wait_ge(xs_ready, at_z(it, 1, 0, Z))
                        if k == 2:
                            pe.wait_ge(e_copied, at_z(it, 1, 0, Z))
                        if k == 3:
                            pe.wait_ge(e_joined, at_z(it, K - 1, 0, Z))
                        mm(zbank(Z)[:, k % 2, :], big_ident[:, :], mask[:, Z, k, :], start=True, stop=False)
                        for g in range(G):
                            last = mm(zbank(Z)[:, k % 2, cols(g)], x_t[:, Z, cols(g)], xs_t[:, Z, k, cols(g)],
                                      start=False, stop=(g == G - 1))
                        last.then_inc(e_ready, 1)
                transpose_p(it, UE, 0)
                for Z in ZS:
                    pe.wait_ge(pt_copied, at_z(it, U, UE, Z))
                    for g in range(G):
                        m = (g % 2) * (P + 1)
                        last = mm(zbank(Z)[:, g // 2, m:m + P + 1], prob_t[:, Z, UE % H, cols(g)], x2[:, Z, g, :],
                                  start=True, stop=True)
                    last.then_inc(o_ready, 1)

                transpose_x(it, 2, lambda Z, g: x13[:, Z, cols(g)])
                values_and_rows(it, 1, one_w_t[:, :], v_one[:, :])
                for Z in ZS:
                    pe.wait_ge(f_copied, at_z(it, 2, 1, Z))
                    pe.wait_ge(rows_lo_ready, at_z(it, 2, 1, Z))
                    gat_scores(it, Z, 0, K, 0, 1)
                transpose_p(it, UO, 0)
                for Z in ZS:
                    pe.wait_ge(pt_copied, at_z(it, U, UO, Z))
                    for g in range(G):
                        m = (g % 2) * (P + 1)
                        last = mm(zbank(Z)[:, g // 2, m:m + P + 1], prob_t[:, Z, UO % H, cols(g)], f3(Z, g),
                                  start=True, stop=True)
                    last.then_inc(o_ready, 1)


_INS = ['x', 'adj', 'L0_gnn_weight', 'L0_gnn_w_ih', 'L0_gnn_w_hh', 'L0_gnn_b_ih', 'L0_gnn_b_hh', 'L1_gnn_W',
        'L1_gnn_b', 'L1_gnn_a', 'L2_gnn_a0', 'L2_gnn_a1', 'L2_gnn_a2', 'L2_gnn_a3', 'L3_gnn_W', 'L3_gnn_a']


def kernel(**inputs):
    import numpy as np
    import concourse.bacc as bacc
    from concourse.bass_utils import run_bass_kernel_spmd

    nc = bacc.Bacc("TRN2", target_bir_lowering=False, num_devices=1)
    arrays, aps = {}, {}
    for name in _INS:
        a = np.ascontiguousarray(inputs[name])
        arrays[f"in_{name}"] = a
        aps[name] = nc.dram_tensor(f"in_{name}", a.shape, mybir.dt.from_np(a.dtype), kind="ExternalInput").ap()
    out = nc.dram_tensor("out_x", inputs["x"].shape, F32, kind="ExternalOutput").ap()
    a = aps
    program(nc, a['x'], a['adj'], a['L0_gnn_weight'], a['L0_gnn_w_ih'], a['L0_gnn_w_hh'], a['L0_gnn_b_ih'],
            a['L0_gnn_b_hh'], a['L1_gnn_W'], a['L1_gnn_b'], a['L1_gnn_a'],
            [a[f'L2_gnn_a{k}'] for k in range(4)], a['L3_gnn_W'], a['L3_gnn_a'], out)
    r = run_bass_kernel_spmd(nc, [arrays], core_ids=[0])
    return r.results[0]["out_x"]
```

```python
from contextlib import ExitStack

import concourse.bass as bass
from concourse import mybir

F32 = mybir.dt.float32
F32R = mybir.dt.float32r
BF16 = mybir.dt.bfloat16
I32 = mybir.dt.int32
ALU = mybir.AluOpType
ACT = mybir.ActivationFunctionType
AX = mybir.AxisListType

P = 128
G = 4
W = G * P
EPS = 1e-5
SLOPE = 0.2
BIG = 2.0 ** 100
XS = (0, 1)
ZS = (0, 1, 2, 3)
NZ = len(ZS)


def at(it, per, k):
    return it * per + k


POOL_TURN = [
    (2, "keep"),
]
ACT_TURN = [
    (1, "high_q"), (2, "n"), (2, "high_h"), (0, "high_hn"), (0, "copy_x"), (1, "r"), (1, "z"), (1, "not_z"),
]
DVE_TURN = [
    (0, "edges"), (1, "low_q"), (2, "take"), (2, "h_new"), (2, "low_h"), (0, "low_hn"), (0, "low_x"),
    (2, "store_y"), (1, "gate_h"), (1, "gate_sum"),
]
PE_TURN = [
    (0, "transpose_x"), (1, "new_r"), (1, "new_n"), (2, "transpose_result"), (0, "transpose_h"), (1, "new_z"),
    (0, "old_r"), (0, "aggregate"), (0, "old_n"), (0, "old_z"),
]
OLDEST_TURN = 2

POOL_ORDER = [
    (1, "subtract", 3), (2, "scale_x", 3), (0, "deviation", 0), (2, "subtract", 4), (1, "residual", 0),
    (3, "subtract", 5), (1, "deviation", 1), (0, "bias", 0), (2, "deviation", 2), (0, "subtract", 0),
    (1, "scale_x", 1), (1, "scale_x", 2), (0, "subtract", 1), (3, "deviation", 3), (0, "subtract", 2),
]
ACT_ORDER = [
    (3, "copy_values", 1), (1, "copy_p", 2), (1, "exponential", 3), (3, "copy_s", 1), (1, "copy_p", 3),
    (3, "high_rows", 1), (4, "normalise", 3), (0, "normalise", 0), (2, "exponential", 4), (3, "scale", 5),
    (0, "copy_x", 0), (2, "copy_p", 4), (0, "copy_values", 0), (0, "copy_s", 0), (3, "exponential", 5),
    (0, "high_rows", 0), (3, "copy_p", 5), (1, "normalise", 1), (0, "scale", 0), (1, "copy_x", 1),
    (1, "scale_x", 0), (0, "scale", 1), (2, "normalise", 2), (0, "exponential", 0), (0, "scale", 2),
    (1, "copy_edge", 0), (0, "copy_p", 0), (0, "exponential", 1), (0, "scale", 3), (2, "copy_x", 2),
    (0, "copy_p", 1), (0, "exponential", 2),
]
DVE_ORDER = [
    (0, "statistics", 0), (2, "join", 1), (0, "moments", 0), (0, "masks", 0), (2, "join", 2),
    (3, "low_rows", 1), (0, "shift", 0), (2, "join", 3), (2, "leaky", 4), (2, "maxima", 4), (3, "expand", 1),
    (1, "inverse", 0), (1, "divide", 0), (3, "leaky", 5), (3, "maxima", 5), (1, "statistics", 1),
    (1, "moments", 1), (2, "inverse", 1), (2, "divide", 1), (0, "low_rows", 0), (1, "shift", 1),
    (0, "expand", 0), (2, "statistics", 2), (2, "moments", 2), (0, "leaky", 0), (0, "maxima", 0),
    (3, "inverse", 2), (2, "shift", 2), (3, "divide", 2), (0, "leaky", 1), (0, "maxima", 1),
    (3, "statistics", 3), (0, "leaky", 2), (3, "moments", 3), (0, "maxima", 2), (0, "leaky", 3),
    (3, "shift", 3), (0, "maxima", 3),
]
PE_ORDER = [
    (1, "transpose_p", 2), (2, "edge_scores", 2), (1, "transpose_p", 3), (3, "transpose_s", 1),
    (2, "edge_scores", 3), (1, "mix_heads", 0), (1, "mix_heads", 1), (1, "mix_heads", 2), (1, "mix_heads", 3),
    (3, "scores", 5), (0, "transpose", 0), (2, "transpose_p", 4), (0, "values", 0), (2, "mix", 1),
    (0, "transpose_s", 0), (3, "transpose_p", 5), (0, "scores", 0), (1, "transpose", 1), (3, "mix", 2),
    (0, "scores", 1), (1, "edge_scores", 0), (0, "scores", 2), (2, "transpose", 2), (0, "transpose_p", 0),
    (0, "scores", 3), (0, "transpose_p", 1), (1, "edge_scores", 1), (2, "values", 1),
]
OLDEST = 4


def program(nc, x, adj, ggnn_w, w_ih, w_hh, b_ih, b_hh, gat_w, gat_b, gat_a, edge_a, one_w, one_a, out):
    B, N, D = x.shape
    L = ggnn_w.shape[0]
    H = gat_a.shape[0]
    C = D // H
    K = len(edge_a)
    PAIRS = B // (2 * G)
    SETS = B // (NZ * G)
    U = H + 2
    UE, UO = H, H + 1
    S = 2 * H
    LOW = G * S
    R = 2 * LOW
    VW = (H * (C + 1) + S, P + 1 + S)
    assert OLDEST_TURN < 2 * L - 1
    assert N == P and D == P and B % (NZ * G) == 0 and K == 4 and H == 4 and L == 3 and 2 * S + 2 <= P and LOW == 32

    with ExitStack() as ctx:
        def sb(name, shape, dt=F32):
            return ctx.enter_context(nc.sbuf_tensor(name, shape, dt))

        def sem(name):
            return ctx.enter_context(nc.semaphore(name))

        def sems(name):
            return [sem(f"{name}_{g}") for g in "ab"]

        def sems_z(name):
            return [sem(f"{name}_{Z}") for Z in ZS]

        ctx.enter_context(nc.allow_non_contiguous_dma(reason="small columns of biases and vectors"))

        bank = [ctx.enter_context(nc.psum_tensor(f"bank_{g}", [P, 4, W], F32)) for g in "ab"]

        def zbank(Z):
            return bank[Z // 2][:, 2 * (Z % 2):2 * (Z % 2) + 2, :]

        I_IH, I_W, I_GAT, I_ONE, I_HH = 0, 3, 3 + L, 4 + L, 5 + L
        NW, N_T = I_HH + 3, I_GAT
        IN_VECTORS = 2 + 2 * H + 1 + 1

        ident = sb("ident", [P, P])
        big_ident = sb("big_ident", [P, P], BF16)
        gat_w_t = sb("gat_w_t", [P, VW[0]])
        one_w_t = sb("one_w_t", [P, VW[1]])
        cw_hi = sb("cw_hi", [P, L, 3 * P], F32R)
        cw_lo = sb("cw_lo", [P, L, 3 * P], F32R)
        hw_hi = sb("hw_hi", [P, 3 * P], F32R)
        hw_lo = sb("hw_lo", [P, 3 * P], F32R)
        b_ih_c = sb("b_ih_c", [P, 3])
        b_hh_c = sb("b_hh_c", [P, 3])
        b_gate = sb("b_gate", [P, 3])
        nb_z = sb("nb_z", [P, 1])
        a_src = sb("a_src", [P, 1])
        a_dst = sb("a_dst", [P, 1])
        gat_b_c = sb("gat_b_c", [P, 1])
        one_a_c = sb("one_a_c", [P, 2])
        edge_a_c = sb("edge_a_c", [P, K])
        sel_1 = sb("sel_1", [R, LOW])
        sel_sum = sb("sel_sum", [R, S + G])
        sel_src = sb("sel_src", [R, H, W], F32R)
        sel_dst = sb("sel_dst", [R, H, P], F32R)
        own = sb("own", [R, W])
        c_rows = sb("c_rows", [R, 2])
        b_row = sb("b_row", [P, P])
        eps = sb("eps", [P, G])
        minus_half = sb("minus_half", [P, G])
        tick = sb("tick", [P, 2 * NZ])

        y_all = sb("y_all", [P, B * D])

        typ_in = sb("typ_in", [P, NZ, W], I32)
        mask = sb("mask", [P, NZ, K + 1, W], BF16)
        stats = sb("stats", [P, NZ, 4, G, 6])
        mv = sb("mv", [P, NZ, 4, G, 2])
        ve = sb("ve", [P, NZ, 4, G])
        rstd = sb("rstd", [P, NZ, 4, G])
        nmr = sb("nmr", [P, NZ, 4, G])
        top = sb("top", [P, NZ, U, G])
        rden = sb("rden", [P, NZ, 3, H * G])
        adj_in = typ_in[:, 0:2, :]

        with ExitStack() as making:
            def sb_0(name, shape, dt=F32):
                return making.enter_context(nc.sbuf_tensor(name, shape, dt))

            w_raw = sb_0("w_raw", [P, NW, P])
            w_t = sb_0("w_t", [P, N_T, P])
            a_wide = sb_0("a_wide", [P, S])
            one_wide = sb_0("one_wide", [P, S])
            a_rows = sb_0("a_rows", [P, R])
            b_and_0 = sb_0("b_and_0", [P, 2])
            b_diag = sb_0("b_diag", [P, P])
            ones = sb_0("ones", [P, P])

        with ExitStack() as part_1:
            def sb_1(name, shape, dt=F32):
                return part_1.enter_context(nc.sbuf_tensor(name, shape, dt))

            clear = sb_1("clear", [P, (NW + N_T + 2) * P + 2 * S + R + 2])
            x_in = sb_1("x_in", [P, 2, W])
            edges = sb_1("edges", [P, 2, W], F32R)
            x_t1 = sb_1("x_t1", [P, 2, W])
            xt_hi = sb_1("xt_hi", [P, 2, W], F32R)
            xt_lo = sb_1("xt_lo", [P, 2, W], F32R)
            h_t = sb_1("h_t", [P, 2, W])
            h_hi = sb_1("h_hi", [P, 2, W], F32R)
            h_lo = sb_1("h_lo", [P, 2, W], F32R)
            hn_hi = sb_1("hn_hi", [P, 2, W], F32R)
            hn_lo = sb_1("hn_lo", [P, 2, W], F32R)
            q_hi = sb_1("q_hi", [P, 2, W], F32R)
            q_lo = sb_1("q_lo", [P, 2, W], F32R)
            r_g = sb_1("r_g", [P, 2, W])
            z_g = sb_1("z_g", [P, 2, W])
            nz_g = sb_1("nz_g", [P, 2, W])
            zh = sb_1("zh", [P, 2, W])
            rn = sb_1("rn", [P, 2, W])
            npre = sb_1("npre", [P, 2, W])
            n_g = sb_1("n_g", [P, 2, W])
            nzn = sb_1("nzn", [P, 2, W])

        x13 = sb("x13", [P, NZ, W])
        x2 = sb("x2", [P, NZ, G, P + 1])
        x_t = sb("x_t", [P, NZ, W])
        y = sb("y", [P, NZ, W])
        fv = sb("fv", [P, NZ, G * H * (C + 1)])
        s_node = sb("s_node", [P, NZ, P])
        s_rows = sb("s_rows", [R, NZ, P], F32R)
        s_own = sb("s_own", [R, NZ, W], F32R)
        score = sb("score", [P, NZ, H, W])
        prob_t = sb("prob_t", [P, NZ, H, W])
        x4 = score[:, :, 2, :]
        mixed = x_t
        xs_t = prob_t

        def f1(Z, g, h):
            return fv[:, Z, (g * H + h) * (C + 1):(g * H + h + 1) * (C + 1)]

        def f3(Z, g):
            return fv[:, Z, g * (P + 1):(g + 1) * (P + 1)]

        weights_in = sem("weights_in")
        vectors_in = sem("vectors_in")
        edge_in = sem("edge_in")
        const_pool = sem("const_pool")
        const_dve = sem("const_dve")
        const_pe = sem("const_pe")
        const_act = sem("const_act")
        chain_sem = sem("chain_sem")

        x_loaded = sem("x_loaded")
        adj_loaded = sem("adj_loaded")
        resid_loaded = sem("resid_loaded")
        edges_ready = sems("edges_ready")
        xtr_ready = sems("xtr_ready")
        xt_hi_ready = sems("xt_hi_ready")
        xt_lo_ready = sems("xt_lo_ready")
        tr_ready = sems("tr_ready")
        h_hi_ready = sems("h_hi_ready")
        h_lo_ready = sems("h_lo_ready")
        hn_hi_ready = sems("hn_hi_ready")
        hn_lo_ready = sems("hn_lo_ready")
        q_ready = sems("q_ready")
        q_hi_ready = sems("q_hi_ready")
        q_lo_ready = sems("q_lo_ready")
        gates_ready = sems("gates_ready")
        r_ready = sems("r_ready")
        z_ready = sems("z_ready")
        nz_ready = sems("nz_ready")
        rn_ready = sems("rn_ready")
        npre_ready = sems("npre_ready")
        n_ready = sems("n_ready")
        zh_ready = sems("zh_ready")
        nzn_ready = sems("nzn_ready")
        h_new = sems("h_new")
        y_stored = sems("y_stored")

        typ_loaded = sems_z("typ_loaded")
        masks_ready = sems_z("masks_ready")
        ln_dve = sems_z("ln_dve")
        ln_pool = sems_z("ln_pool")
        x_normed = sems_z("x_normed")
        xt_ready = sems_z("xt_ready")
        xs_ready = sems_z("xs_ready")
        xt_copied = sems_z("xt_copied")
        f_ready = sems_z("f_ready")
        f_copied = sems_z("f_copied")
        rows_lo_ready = sems_z("rows_lo_ready")
        u_ready = sems_z("u_ready")
        e_ready = sems_z("e_ready")
        e_joined = sems_z("e_joined")
        t_ready = sems_z("t_ready")
        top_ready = sems_z("top_ready")
        sub_ready = sems_z("sub_ready")
        p_ready = sems_z("p_ready")
        pt_ready = sems_z("pt_ready")
        pt_copied = sems_z("pt_copied")
        o_ready = sems_z("o_ready")
        divided = sems_z("divided")
        y_ready = sems_z("y_ready")
        out_stored = sems_z("out_stored")

        def g4(ap):
            return ap.rearrange("p (g n) -> p g n", g=G)

        def cols(g):
            return slice(g * P, (g + 1) * P)

        def y1_at(it, X):
            return y_all[:, bass.ds(it * (2 * W) + X * W, W)]

        def y2_graph(it, Z, g):
            return y_all[:, bass.ds(it * (NZ * W) + Z * W + g * P, P)]

        def graphs(dram, it, n):
            return dram[bass.ds(it * n, n), :, :].rearrange("b n d -> n b d")

        def tiles(tile):
            return tile.rearrange("p x (g n) -> p (x g) n", g=G)

        def part_2_beats(engine, order, step):
            def beats(it, count, first, last):
                for beat in range(count):
                    for age, name, n in order:
                        sets_back = (age - beat + NZ - 1) // NZ
                        if sets_back > 0 and first or sets_back == 0 and last:
                            continue
                        step(name, n, (beat - age) % NZ, it - sets_back if sets_back else it)

            beats(0, NZ, True, False)
            with engine.Fori(1, SETS) as it:
                beats(it, NZ, False, False)
            beats(SETS, OLDEST, False, True)

        def part_1_turns(engine, order, step):
            def turns(it, count, first, last):
                for turn in range(count):
                    for age, name in order:
                        pairs_back = (age - turn + 2 * L - 1) // (2 * L)
                        if pairs_back > 0 and first or pairs_back == 0 and last:
                            continue
                        slot = (turn - age) % (2 * L)
                        step(name, slot % 2, slot // 2, it - pairs_back if pairs_back else it)

            turns(0, 2 * L, True, False)
            with engine.Fori(1, PAIRS) as it:
                turns(it, 2 * L, False, False)
            turns(PAIRS, OLDEST_TURN, False, True)

        def later(it):
            return not isinstance(it, int) or it > 0

        def products(Z, n):
            return zbank(Z)[:, :, 0:2 * VW[n]].rearrange("p b (q v) -> p b q v", v=VW[n])

        block = ctx.enter_context(nc.Block())

        @block.sync
        def _(sp):
            sp.dma_start(w_raw[:, I_IH:I_IH + 3, :], w_ih.rearrange("(g o) i -> o g i", g=3)).then_inc(weights_in, 16)
            sp.dma_start(w_raw[:, I_W:I_W + L, :], ggnn_w.rearrange("l d e -> d l e")).then_inc(weights_in, 16)
            sp.dma_start(w_raw[:, I_GAT, :], gat_w).then_inc(weights_in, 16)
            sp.dma_start(w_raw[:, I_ONE, :], one_w).then_inc(weights_in, 16)
            sp.dma_start(w_raw[:, I_HH:I_HH + 3, :], w_hh.rearrange("(g o) i -> o g i", g=3)).then_inc(weights_in, 16)

            def load_pair(it):
                sp.dma_start(tiles(x_in[:, :, :]), graphs(x, it, 2 * G)).then_inc(x_loaded, 16)
                sp.dma_start(tiles(adj_in), graphs(adj, it, 2 * G)).then_inc(adj_loaded, 16)
                sp.dma_start(y_all[:, bass.ds(it * (2 * W), 2 * W)].rearrange("p (b d) -> p b d", d=D),
                             graphs(x, it, 2 * G)).then_inc(resid_loaded, 16)

            for h in range(H):
                head = slice(h * C, (h + 1) * C)
                sp.dma_start(a_src[head, :], gat_a[h, 0:C].rearrange("(c o) -> c o", o=1)).then_inc(vectors_in, 16)
                sp.dma_start(a_dst[head, :], gat_a[h, C:2 * C].rearrange("(c o) -> c o", o=1)).then_inc(vectors_in, 16)
            load_pair(0)
            for k in range(K):
                sp.dma_start(edge_a_c[:, k:k + 1], edge_a[k].rearrange("(c o) -> c o", o=1)).then_inc(edge_in, 16)
            with sp.Fori(1, PAIRS) as it:
                for X in XS:
                    sp.wait_ge(xtr_ready[X], it)
                    sp.wait_ge(hn_lo_ready[X], at(it - 1, L, 1))
                    sp.wait_ge(edges_ready[X], it)
                sp.wait_ge(resid_loaded, at(it - 1, 16, 16))
                load_pair(it)

            def load_types(it, Z):
                sp.dma_start(g4(typ_in[:, Z, :]), adj[bass.ds(it * (NZ * G) + Z * G, G), :, :].rearrange("b n d -> n b d")
                             ).then_inc(typ_loaded[Z], 16)

            def store_group(it, Z):
                sp.wait_ge(x_normed[Z], at(it, 4, 4))
                sp.dma_start(out[bass.ds(it * (NZ * G) + Z * G, G), :, :].rearrange("b n d -> n b d"),
                             g4(x4[:, Z, :])).then_inc(out_stored[Z], 16)

            for X in XS:
                sp.wait_ge(edges_ready[X], PAIRS)
            for Z in ZS:
                load_types(0, Z)
            with sp.Fori(1, SETS) as it:
                for Z in ZS:
                    sp.wait_ge(masks_ready[Z], it)
                    load_types(it, Z)
                for Z in ZS:
                    store_group(it - 1, Z)
            for Z in ZS:
                store_group(SETS - 1, Z)
            for Z in ZS:
                sp.wait_ge(out_stored[Z], 16 * (SETS + 1))

        @block.gpsimd
        def _(pool):
            nc.gpsimd.memset(ident[:, :], 1.0).then_inc(const_pool, 1)
            pool.wait_ge(const_pool, 1)
            nc.gpsimd.affine_select(out=ident[:, :], in_=ident[:, :], compare_op=ALU.is_equal, fill=0.0,
                                    base=0, pattern=[[-1, P]], channel_multiplier=1).then_inc(const_pool, 1)
            nc.gpsimd.memset(eps[:, :], EPS)
            nc.gpsimd.memset(minus_half[:, :], -0.5).then_inc(const_pool, 1)

            def turn_step(name, X, l, it):
                if name == "keep":
                    pool.wait_ge(z_ready[X], at(it, L, l + 1))
                    if l == 0:
                        pool.wait_ge(xt_hi_ready[X], at(it, 1, 1))
                    else:
                        pool.wait_ge(h_new[X], at(it, L, l))
                    old = x_t1 if l == 0 else h_t
                    nc.gpsimd.tensor_tensor(zh[:, X, :], z_g[:, X, :], old[:, X, :], ALU.mult).then_inc(zh_ready[X], 1)

            part_1_turns(pool, POOL_TURN, turn_step)

            pool.wait_ge(edge_in, 16 * K)

            def step(name, n, Z, it):
                if name == "deviation":
                    pool.wait_ge(ln_dve[Z], at(it, 12, 3 * n + 2))
                    nc.gpsimd.tensor_tensor(ve[:, Z, n, :], mv[:, Z, n, :, 1], eps[:, :], ALU.add).then_inc(ln_pool[Z], 1)
                    pool.wait_ge(ln_pool[Z], at(it, 8, 2 * n + 1))
                    nc.gpsimd.tensor_tensor(rstd[:, Z, n, :], ve[:, Z, n, :], minus_half[:, :],
                                            ALU.pow).then_inc(ln_pool[Z], 1)
                elif name == "scale_x":
                    pool.wait_ge(xt_copied[Z], at(it, 4, 2))
                    nc.gpsimd.tensor_tensor(xs_t[:, Z, n, :], x_t[:, Z, :], edge_a_c[:, n:n + 1].to_broadcast([P, W]),
                                            ALU.mult).then_inc(xs_ready[Z], 1)
                elif name == "bias":
                    pool.wait_ge(x_normed[Z], at(it, 4, 1))
                    nc.gpsimd.tensor_tensor(g4(y[:, Z, :]), g4(x13[:, Z, :]),
                                            b_row[:, :].unsqueeze(1).to_broadcast([P, G, P]),
                                            ALU.add).then_inc(y_ready[Z], 1)
                elif name == "subtract":
                    s = g4(score[:, Z, n % H, :])
                    pool.wait_ge(top_ready[Z], at(it, 2 * U, 2 * n + 2))
                    nc.gpsimd.tensor_tensor(s, s, top[:, Z, n, :].unsqueeze(2).to_broadcast([P, G, P]),
                                            ALU.subtract).then_inc(sub_ready[Z], 1)
                elif name == "residual":
                    pool.wait_ge(y_ready[Z], at(it, 4, 1))
                    pool.wait_ge(divided[Z], at(it, 4, 2))
                    nc.gpsimd.tensor_tensor(y[:, Z, :], mixed[:, Z, :], y[:, Z, :], ALU.add).then_inc(y_ready[Z], 1)

            part_2_beats(pool, POOL_ORDER, step)

        @block.scalar
        def _(act):
            act.dma_start(b_ih_c[:, :], b_ih.rearrange("(g o) -> o g", g=3)).then_inc(vectors_in, 16)
            act.dma_start(b_hh_c[:, :], b_hh.rearrange("(g o) -> o g", g=3)).then_inc(vectors_in, 16)
            act.dma_start(gat_b_c[:, :], gat_b.rearrange("(c o) -> c o", o=1)).then_inc(vectors_in, 16)
            act.dma_start(one_a_c[:, :], one_a.rearrange("a (s c) -> c (a s)", s=2)).then_inc(vectors_in, 16)

            act.wait_ge(const_pe, 1)
            nc.scalar.copy(w_t[:, 0:4, :].rearrange("p w o -> p (w o)"), bank[0][:, 0, :])
            nc.scalar.copy(w_t[:, 4:N_T, :].rearrange("p w o -> p (w o)"),
                           bank[0][:, 1, 0:(N_T - 4) * P]).then_inc(const_act, 1)
            act.wait_ge(const_dve, 1)
            nc.scalar.copy(gat_w_t[:, 0:H * (C + 1)].rearrange("p (h c) -> p h c", c=C + 1)[:, :, 0:C],
                           bank[0][:, 1, cols(I_GAT - 4)].rearrange("p (h c) -> p h c", c=C))
            nc.scalar.copy(one_w_t[:, 0:P], bank[0][:, 1, cols(I_ONE - 4)])
            nc.scalar.copy(hw_hi[:, :], bank[0][:, 2, 0:3 * P]).then_inc(const_act, 1)
            for l in range(L):
                act.wait_ge(const_pe, 2 + l)
                nc.scalar.copy(cw_hi[:, l, :], bank[1][:, l, 0:3 * P]).then_inc(const_act, 1)

            def turn_step(name, X, l, it):
                RB, ZB, IN, HN = (bank[X][:, b, :] for b in range(4))
                if name == "copy_x" and l == 0:
                    act.wait_ge(xtr_ready[X], at(it, 1, 1))
                    nc.scalar.copy(x_t1[:, X, :], HN)
                    nc.scalar.copy(xt_hi[:, X, :], HN).then_inc(xt_hi_ready[X], 1)
                elif name == "high_hn":
                    if l == 0:
                        act.wait_ge(x_loaded, at(it, 16, 16))
                    else:
                        act.wait_ge(tr_ready[X], at(it, L, l))
                    nc.scalar.copy(hn_hi[:, X, :], x_in[:, X, :] if l == 0 else HN).then_inc(hn_hi_ready[X], 1)
                elif name == "high_h" and l + 1 < L:
                    act.wait_ge(h_new[X], at(it, L, l + 1))
                    nc.scalar.copy(h_hi[:, X, :], h_t[:, X, :]).then_inc(h_hi_ready[X], 1)
                elif name == "high_q":
                    act.wait_ge(q_ready[X], at(it, L, l + 1))
                    nc.scalar.copy(q_hi[:, X, :], IN).then_inc(q_hi_ready[X], 1)
                elif name == "r":
                    act.wait_ge(gates_ready[X], at(it, 3 * L, 3 * l + 1))
                    nc.scalar.activation(r_g[:, X, :], RB, ACT.Sigmoid, bias=b_gate[:, 0:1]).then_inc(r_ready[X], 1)
                elif name == "n":
                    act.wait_ge(npre_ready[X], at(it, L, l + 1))
                    nc.scalar.activation(n_g[:, X, :], npre[:, X, :], ACT.Tanh, bias=b_ih_c[:, 2:3]).then_inc(n_ready[X], 1)
                elif name == "z":
                    act.wait_ge(gates_ready[X], at(it, 3 * L, 3 * l + 3))
                    nc.scalar.activation(z_g[:, X, :], ZB, ACT.Sigmoid, bias=b_gate[:, 1:2]).then_inc(z_ready[X], 1)
                elif name == "not_z":
                    act.wait_ge(gates_ready[X], at(it, 3 * L, 3 * l + 3))
                    nc.scalar.activation(nz_g[:, X, :], ZB, ACT.Sigmoid, bias=nb_z[:, 0:1],
                                         scale=-1.0).then_inc(nz_ready[X], 1)

            act.wait_ge(const_dve, 2)
            part_1_turns(act, ACT_TURN, turn_step)

            act.wait_ge(edge_in, 16 * K)
            act.wait_ge(const_dve, 5)

            def step(name, n, Z, it):
                b0, b1 = zbank(Z)[:, 0, :], zbank(Z)[:, 1, :]
                if name == "normalise":
                    act.wait_ge(ln_dve[Z], at(it, 12, 3 * n + 3))
                    if n == 0:
                        nc.scalar.copy(tick[:, Z:Z + 1], minus_half[:, 0:1])
                    for g in range(G):
                        src = y2_graph(it, Z, g) if n == 0 else y[:, Z, cols(g)]
                        dst = (x13[:, Z, cols(g)], x2[:, Z, g, 0:P], x13[:, Z, cols(g)], x4[:, Z, cols(g)])[n]
                        last = nc.scalar.activation(dst, src, ACT.Identity, bias=nmr[:, Z, n, g:g + 1],
                                                    scale=rstd[:, Z, n, g:g + 1])
                    last.then_inc(x_normed[Z], 1)
                elif name == "copy_x":
                    act.wait_ge(xt_ready[Z], at(it, 3, n + 1))
                    nc.scalar.copy(x_t[:, Z, :], b0).then_inc(xt_copied[Z], 1)
                elif name == "copy_values":
                    v = VW[n] - S
                    act.wait_ge(f_ready[Z], at(it, 4, 2 * n + 1))
                    nc.scalar.copy(fv[:, Z, 0:G * v].rearrange("p (b q v) -> p b q v", b=2, v=v),
                                   products(Z, n)[:, :, :, 0:v]).then_inc(f_copied[Z], 1)
                elif name == "copy_s":
                    for twice in range(2):
                        last = nc.scalar.copy(s_node[:, Z, twice * LOW:(twice + 1) * LOW].rearrange("p (b q s) -> p b q s", b=2, s=S),
                                              products(Z, n)[:, :, :, VW[n] - S:VW[n]])
                    last.then_inc(f_copied[Z], 1)
                elif name == "high_rows":
                    act.wait_ge(f_ready[Z], at(it, 4, 2 * n + 2))
                    nc.scalar.activation(s_rows[:, Z, :], b1[0:R, 0:P], ACT.Identity,
                                         bias=c_rows[:, n:n + 1]).then_inc(f_copied[Z], 1)
                elif name == "scale_x":
                    act.wait_ge(xt_copied[Z], at(it, 4, 2))
                    nc.scalar.mul(xs_t[:, Z, n, :], x_t[:, Z, :], edge_a_c[:, n:n + 1]).then_inc(xt_copied[Z], 1)
                elif name == "copy_edge":
                    act.wait_ge(e_ready[Z], at(it, K, 1))
                    nc.scalar.copy(score[:, Z, UE % H, :], b0).then_inc(t_ready[Z], 1)
                elif name == "scale":
                    act.wait_ge(u_ready[Z], at(it, H + 1, min(n, H) + 1))
                    if n == 2:
                        act.wait_ge(out_stored[Z], at(it, 16, 16))
                    nc.scalar.mul(score[:, Z, n % H, :], b0, SLOPE).then_inc(t_ready[Z], 1)
                elif name == "exponential":
                    act.wait_ge(sub_ready[Z], at(it, U, n + 1))
                    nc.scalar.activation(score[:, Z, n % H, :], score[:, Z, n % H, :], ACT.Exp).then_inc(p_ready[Z], 1)
                elif name == "copy_p":
                    act.wait_ge(pt_ready[Z], at(it, U, n + 1))
                    nc.scalar.copy(prob_t[:, Z, n % H, :], b1).then_inc(pt_copied[Z], 1)

            part_2_beats(act, ACT_ORDER, step)

        @block.vector
        def _(dve):
            V = nc.vector
            V.memset(ones[:, :], 1.0)
            V.memset(one_wide[:, :], 0.0)
            V.memset(gat_w_t[:, :], 0.0)
            V.memset(one_w_t[:, :], 0.0)
            V.memset(b_and_0[:, :], 0.0)
            V.memset(a_wide[:, :], 0.0).then_inc(const_dve, 1)
            for Z in ZS:
                V.memset(tick[:, NZ + Z:NZ + Z + 1], 0.0).then_inc(out_stored[Z], 16)
            dve.wait_ge(const_dve, 1)
            dve.wait_ge(const_pool, 3)
            dve_step = [0]

            def chain(ins):
                dve_step[0] += 1
                ins.then_inc(chain_sem, 1)
                dve.wait_ge(chain_sem, dve_step[0])

            chain(V.tensor_tensor(sel_1[:, :], ident[0:R, 0:LOW], ident[0:R, LOW:R], ALU.add))
            chain(V.tensor_reduce(sel_sum[:, 0:S], sel_1[:, :].rearrange("p (g s) -> p s g", s=S), AX.X, ALU.add))
            chain(V.tensor_reduce(sel_sum[:, S:S + G], sel_1[:, :].rearrange("p (g s) -> p g s", s=S), AX.X, ALU.add))
            for h in range(H):
                V.tensor_copy(g4(sel_src[:, h, :]), sel_1[:, :].rearrange("p (g s) -> p g s", s=S)[:, :, h:h + 1]
                              .to_broadcast([R, G, P]))
                V.tensor_copy(sel_dst[:, h, :], sel_sum[:, H + h:H + h + 1].to_broadcast([R, P]))
            V.tensor_copy(g4(own[:, :]), sel_sum[:, S:S + G].unsqueeze(2).to_broadcast([R, G, P]))
            V.tensor_scalar(big_ident[:, :], ident[:, :], BIG, None, ALU.mult)
            dve.wait_ge(vectors_in, 16 * IN_VECTORS)
            chain(V.tensor_tensor(b_gate[:, :], b_ih_c[:, :], b_hh_c[:, :], ALU.add))
            V.tensor_scalar(nb_z[:, :], b_gate[:, 1:2], -1.0, None, ALU.mult).then_inc(const_dve, 1)
            for h in range(H):
                head = slice(h * C, (h + 1) * C)
                V.tensor_copy(a_wide[head, h:h + 1], a_src[head, :])
                last = V.tensor_copy(a_wide[head, H + h:H + h + 1], a_dst[head, :])
            chain(last)
            V.tensor_copy(a_rows[:, :].rearrange("p (m s) -> p m s", s=S), a_wide[:, :].unsqueeze(1).to_broadcast([P, 2 * G, S]))
            V.tensor_copy(one_wide[:, 0:H + 1:H], one_a_c[:, :])
            V.tensor_copy(b_and_0[:, 0:1], gat_b_c[:, :])
            V.tensor_scalar(b_diag[:, :], ident[:, :], gat_b_c[:, 0:1], None, ALU.mult).then_inc(const_dve, 1)
            dve.wait_ge(const_act, 2)
            V.tensor_tensor(hw_lo[:, :], bank[0][:, 2, 0:3 * P], hw_hi[:, :].bitcast(F32),
                            ALU.subtract).then_inc(const_dve, 1)
            for l in range(L):
                dve.wait_ge(const_act, 3 + l)
                V.tensor_tensor(cw_lo[:, l, :], bank[1][:, l, 0:3 * P], cw_hi[:, l, :].bitcast(F32), ALU.subtract)
            dve.wait_ge(const_pe, 2 + L)
            V.tensor_copy(gat_w_t[:, H * (C + 1):VW[0]], bank[1][:, 3, 0:S])
            V.tensor_copy(one_w_t[:, P + 1:VW[1]], bank[1][:, 3, S:2 * S])
            V.tensor_copy(c_rows[:, :], bank[1][0:R, 3, 2 * S:2 * S + 2])
            V.tensor_copy(b_row[:, :], bank[1][:, 3, P:2 * P]).then_inc(const_dve, 1)

            def turn_step(name, X, l, it):
                IN, HN = bank[X][:, 2, :], bank[X][:, 3, :]
                if name == "edges" and l == 0:
                    dve.wait_ge(adj_loaded, at(it, 16, 16))
                    V.tensor_scalar(edges[:, X, :], adj_in[:, X, :], 0.0, None, ALU.not_equal).then_inc(edges_ready[X], 1)
                elif name == "low_x" and l == 0:
                    dve.wait_ge(xt_hi_ready[X], at(it, 1, 1))
                    V.tensor_tensor(xt_lo[:, X, :], x_t1[:, X, :], xt_hi[:, X, :].bitcast(F32),
                                    ALU.subtract).then_inc(xt_lo_ready[X], 1)
                elif name == "low_hn":
                    if l == 0:
                        dve.wait_ge(x_loaded, at(it, 16, 16))
                    dve.wait_ge(hn_hi_ready[X], at(it, L, l + 1))
                    V.tensor_tensor(hn_lo[:, X, :], x_in[:, X, :] if l == 0 else HN, hn_hi[:, X, :].bitcast(F32),
                                    ALU.subtract).then_inc(hn_lo_ready[X], 1)
                elif name == "low_q":
                    dve.wait_ge(q_hi_ready[X], at(it, L, l + 1))
                    V.tensor_tensor(q_lo[:, X, :], IN, q_hi[:, X, :].bitcast(F32), ALU.subtract).then_inc(q_lo_ready[X], 1)
                elif name == "gate_h":
                    dve.wait_ge(r_ready[X], at(it, L, l + 1))
                    V.scalar_tensor_tensor(out=rn[:, X, :], in0=HN, scalar=b_hh_c[:, 2:3], in1=r_g[:, X, :],
                                           op0=ALU.add, op1=ALU.mult).then_inc(rn_ready[X], 1)
                elif name == "gate_sum":
                    dve.wait_ge(rn_ready[X], at(it, L, l + 1))
                    dve.wait_ge(gates_ready[X], at(it, 3 * L, 3 * l + 2))
                    V.tensor_tensor(npre[:, X, :], IN, rn[:, X, :], ALU.add).then_inc(npre_ready[X], 1)
                elif name == "take":
                    dve.wait_ge(nz_ready[X], at(it, L, l + 1))
                    dve.wait_ge(n_ready[X], at(it, L, l + 1))
                    V.tensor_tensor(nzn[:, X, :], nz_g[:, X, :], n_g[:, X, :], ALU.mult).then_inc(nzn_ready[X], 1)
                elif name == "h_new":
                    dve.wait_ge(nzn_ready[X], at(it, L, l + 1))
                    dve.wait_ge(zh_ready[X], at(it, L, l + 1))
                    V.tensor_tensor(h_t[:, X, :], nzn[:, X, :], zh[:, X, :], ALU.add).then_inc(h_new[X], 1)
                elif name == "low_h" and l + 1 < L:
                    dve.wait_ge(h_hi_ready[X], at(it, L - 1, l + 1))
                    V.tensor_tensor(h_lo[:, X, :], h_t[:, X, :], h_hi[:, X, :].bitcast(F32),
                                    ALU.subtract).then_inc(h_lo_ready[X], 1)
                elif name == "store_y" and l + 1 == L:
                    dve.wait_ge(resid_loaded, at(it, 16, 16))
                    dve.wait_ge(tr_ready[X], at(it, L, L))
                    V.tensor_tensor(y1_at(it, X), IN, y1_at(it, X), ALU.add).then_inc(y_stored[X], 1)

            part_1_turns(dve, DVE_TURN, turn_step)

            for Z in ZS:
                V.memset(x2[:, Z, :, P:P + 1], 1.0)
                V.memset(s_node[:, Z, R:P], 0.0)

            def step(name, n, Z, it):
                b0, b1 = zbank(Z)[:, 0, :], zbank(Z)[:, 1, :]
                if name == "statistics":
                    if n:
                        dve.wait_ge(y_ready[Z], at(it, 4, n + 1))
                    for g in range(G):
                        src = y2_graph(it, Z, g) if n == 0 else y[:, Z, cols(g)]
                        last = V.bn_stats(stats[:, Z, n, g, :], src)
                    last.then_inc(ln_dve[Z], 1)
                elif name == "moments":
                    dve.wait_ge(ln_dve[Z], at(it, 12, 3 * n + 1))
                    V.memset(tick[:, NZ + Z:NZ + Z + 1], 0.0)
                    for g in range(G):
                        last = V.bn_aggr(mv[:, Z, n, g, :], stats[:, Z, n, g, :])
                    last.then_inc(ln_dve[Z], 1)
                elif name == "shift":
                    dve.wait_ge(ln_pool[Z], at(it, 8, 2 * n + 2))
                    V.scalar_tensor_tensor(out=nmr[:, Z, n, :], in0=mv[:, Z, n, :, 0], scalar=-1.0, in1=rstd[:, Z, n, :],
                                           op0=ALU.mult, op1=ALU.mult).then_inc(ln_dve[Z], 1)
                elif name == "masks":
                    dve.wait_ge(typ_loaded[Z], at(it, 16, 16))
                    for k in range(K):
                        V.tensor_scalar(mask[:, Z, k, :], typ_in[:, Z, :], float(k + 1), 1.0, ALU.is_equal, ALU.subtract)
                    V.tensor_scalar(mask[:, Z, K, :], typ_in[:, Z, :], 0.0, 1.0, ALU.is_gt,
                                    ALU.subtract).then_inc(masks_ready[Z], 1)
                elif name == "low_rows":
                    v, c = (VW[n] - S, (C, P)[n])
                    dve.wait_ge(f_copied[Z], at(it, 6, 3 * n + 3))
                    V.memset(fv[:, Z, 0:G * v].rearrange("p (m c) -> p m c", c=c + 1)[:, :, c:c + 1], 1.0)
                    V.scalar_tensor_tensor(out=s_rows[LOW:R, Z, :], in0=b1[LOW:R, 0:P], scalar=c_rows[LOW:R, n:n + 1],
                                           in1=s_rows[LOW:R, Z, :].bitcast(F32), op0=ALU.add,
                                           op1=ALU.subtract).then_inc(rows_lo_ready[Z], 1)
                elif name == "expand":
                    dve.wait_ge(rows_lo_ready[Z], at(it, 4, 2 * n + 1))
                    V.tensor_tensor(g4(s_own[:, Z, :]), s_rows[:, Z, :].bitcast(F32).unsqueeze(1).to_broadcast([R, G, P]),
                                    g4(own[:, :]), ALU.mult).then_inc(rows_lo_ready[Z], 1)
                elif name == "join":
                    dve.wait_ge(e_ready[Z], at(it, K, n + 1))
                    if n == 1:
                        dve.wait_ge(t_ready[Z], at(it, U, UE + 1))
                    else:
                        dve.wait_ge(e_joined[Z], at(it, K - 1, n - 1))
                    V.tensor_tensor(score[:, Z, UE % H, :], b1 if n % 2 else b0, score[:, Z, UE % H, :],
                                    ALU.max).then_inc(e_joined[Z], 1)
                elif name == "leaky":
                    if n == UE:
                        dve.wait_ge(e_joined[Z], at(it, K - 1, K - 1))
                        s = score[:, Z, UE % H, :]
                        V.scalar_tensor_tensor(out=s, in0=s, scalar=SLOPE, in1=s, op0=ALU.mult,
                                               op1=ALU.max).then_inc(top_ready[Z], 1)
                    else:
                        dve.wait_ge(t_ready[Z], at(it, U, n + 1))
                        V.tensor_tensor(score[:, Z, n % H, :], b0, score[:, Z, n % H, :],
                                        ALU.max).then_inc(top_ready[Z], 1)
                elif name == "maxima":
                    dve.wait_ge(top_ready[Z], at(it, 2 * U, 2 * n + 1))
                    V.tensor_reduce(top[:, Z, n, :], g4(score[:, Z, n % H, :]), AX.X, ALU.max).then_inc(top_ready[Z], 1)
                elif name == "inverse":
                    dve.wait_ge(o_ready[Z], at(it, 3, n + 1))
                    o, inverse = values_and_sums(Z, n)
                    V.reciprocal(inverse, o[:, :, :, D // (H, 1, 1)[n]]).then_inc(divided[Z], 1)
                elif name == "divide":
                    o, inverse = values_and_sums(Z, n)
                    dve.wait_ge(divided[Z], at(it, 4, (1, 3, 4)[n]))
                    if n == 0:
                        V.tensor_tensor(mixed[:, Z, :].rearrange("p (b m c) -> p b m c", b=2, c=C), o[:, :, :, 0:C],
                                        inverse.unsqueeze(3).to_broadcast([P, 2, 2 * H, C]),
                                        ALU.mult).then_inc(divided[Z], 1)
                    else:
                        for g in range(G):
                            last = V.scalar_tensor_tensor(out=y[:, Z, cols(g)], in0=o[:, g // 2, g % 2, 0:P],
                                                          scalar=rden[:, Z, n, g:g + 1],
                                                          in1=x2[:, Z, g, 0:P] if n == 1 else x13[:, Z, cols(g)],
                                                          op0=ALU.mult, op1=ALU.add)
                        last.then_inc(y_ready[Z], 1)

            def values_and_sums(Z, n):
                heads = (H, 1, 1)[n]
                width = D // heads + 1
                return (zbank(Z)[:, :, 0:2 * heads * width].rearrange("p b (m c) -> p b m c", c=width),
                        rden[:, Z, n, 0:G * heads].rearrange("p (b m) -> p b m", b=2))

            part_2_beats(dve, DVE_ORDER, step)

        @block.tensor
        def _(pe):
            mm = nc.tensor.matmul
            tr = nc.tensor.transpose

            pe.wait_ge(weights_in, 16 * 5)
            pe.wait_ge(const_pool, 3)
            for i in range(NW):
                place = bank[0][:, i // 4, cols(i % 4)] if i < I_HH else bank[0][:, 2, cols(i - I_HH)]
                last = tr(place, w_raw[:, i, :], ident[:, :])
            last.then_inc(const_pe, 1)
            pe.wait_ge(const_act, 1)
            w_ih_t = w_t[:, I_IH:I_IH + 3, :].rearrange("p g o -> p (g o)")
            for l in range(L):
                mm(bank[1][:, l, 0:3 * P], w_t[:, I_W + l, :], w_ih_t, start=True, stop=True).then_inc(const_pe, 1)
            pe.wait_ge(const_dve, 3)
            small = bank[1][:, 3, :]
            mm(small[:, 0:S], w_raw[:, I_GAT, :], a_wide[:, :], start=True, stop=True)
            mm(small[:, S:2 * S], w_raw[:, I_ONE, :], one_wide[:, :], start=True, stop=True)
            mm(small[0:R, 2 * S:2 * S + 2], a_rows[:, :], b_and_0[:, :], start=True, stop=True)
            mm(small[:, P:2 * P], ones[:, :], b_diag[:, :], start=True, stop=True).then_inc(const_pe, 1)
            pe.wait_ge(const_dve, 4)

            def product(dst, w_hi, w_lo, m_hi, m_lo, start, stop):
                mm(dst, w_hi, m_hi, start=start, stop=False)
                mm(dst, w_lo, m_hi, start=False, stop=False)
                return mm(dst, w_hi, m_lo, start=False, stop=stop)

            def transpose_group(dst, src):
                for g in range(G):
                    last = tr(dst[:, cols(g)], src[:, cols(g)], ident[:, :])
                return last

            def turn_step(name, X, l, it):
                RB, ZB, IN, HN = (bank[X][:, b, :] for b in range(4))
                old_hi, old_lo = (xt_hi, xt_lo) if l == 0 else (h_hi, h_lo)
                if name == "transpose_x" and l == 0:
                    pe.wait_ge(x_loaded, at(it, 16, 16))
                    if later(it):
                        pe.wait_ge(rn_ready[X], at(it, L, 0))
                    elif X == 1:
                        pe.wait_ge(const_dve, 5)
                    transpose_group(HN, x_in[:, X, :]).then_inc(xtr_ready[X], 1)
                elif name == "transpose_h" and l > 0:
                    pe.wait_ge(h_new[X], at(it, L, l))
                    transpose_group(HN, h_t[:, X, :]).then_inc(tr_ready[X], 1)
                elif name in ("old_r", "old_z"):
                    if l == 0:
                        pe.wait_ge(xt_lo_ready[X], at(it, 1, 1))
                        if later(it):
                            pe.wait_ge(h_new[X], at(it, L, 0))
                    else:
                        pe.wait_ge(h_lo_ready[X], at(it, L - 1, l))
                    g, dst = (0, RB) if name == "old_r" else (1, ZB)
                    product(dst, hw_hi[:, cols(g)], hw_lo[:, cols(g)], old_hi[:, X, :], old_lo[:, X, :], True, False)
                elif name == "aggregate":
                    pe.wait_ge(hn_lo_ready[X], at(it, L, l + 1))
                    if l == 0:
                        pe.wait_ge(edges_ready[X], at(it, 1, 1))
                        if later(it):
                            pe.wait_ge(y_stored[X], at(it, 1, 0))
                    for g in range(G):
                        mm(IN[:, cols(g)], hn_hi[:, X, cols(g)], edges[:, X, cols(g)], start=True, stop=False)
                        last = mm(IN[:, cols(g)], hn_lo[:, X, cols(g)], edges[:, X, cols(g)], start=False, stop=True)
                    last.then_inc(q_ready[X], 1)
                elif name == "old_n":
                    pe.wait_ge(hn_lo_ready[X], at(it, L, l + 1))
                    product(HN, hw_hi[:, cols(2)], hw_lo[:, cols(2)], old_hi[:, X, :], old_lo[:, X, :], True, True)
                elif name in ("new_r", "new_n", "new_z"):
                    pe.wait_ge(q_lo_ready[X], at(it, L, l + 1))
                    g, dst, start = {"new_r": (0, RB, False), "new_z": (1, ZB, False), "new_n": (2, IN, True)}[name]
                    product(dst, cw_hi[:, l, cols(g)], cw_lo[:, l, cols(g)], q_hi[:, X, :], q_lo[:, X, :],
                            start, True).then_inc(gates_ready[X], 1)
                elif name == "transpose_result" and l + 1 == L:
                    pe.wait_ge(h_new[X], at(it, L, L))
                    transpose_group(IN, h_t[:, X, :]).then_inc(tr_ready[X], 1)

            part_1_turns(pe, PE_TURN, turn_step)

            def step(name, n, Z, it):
                b0, b1 = zbank(Z)[:, 0, :], zbank(Z)[:, 1, :]
                if name == "transpose":
                    pe.wait_ge(x_normed[Z], at(it, 4, n + 1))
                    for g in range(G):
                        last = tr(b0[:, cols(g)], x2[:, Z, g, 0:P] if n == 1 else x13[:, Z, cols(g)], ident[:, :])
                    last.then_inc(xt_ready[Z], 1)
                elif name == "values":
                    pe.wait_ge(xt_copied[Z], at(it, 4, (1, 4)[n]))
                    for g in range(G):
                        last = mm(products(Z, n)[:, g // 2, g % 2, :], x_t[:, Z, cols(g)], (gat_w_t, one_w_t)[n][:, :],
                                  start=True, stop=True)
                    last.then_inc(f_ready[Z], 1)
                elif name == "transpose_s":
                    pe.wait_ge(f_copied[Z], at(it, 6, 3 * n + 2))
                    tr(b1[:, 0:P], s_node[:, Z, :], ident[:, :]).then_inc(f_ready[Z], 1)
                elif name == "scores":
                    m, h = (0, n) if n < H else (K, 0)
                    if n == 0:
                        pe.wait_ge(masks_ready[Z], at(it, 1, 1))
                    if n == 0 or n == UO:
                        pe.wait_ge(rows_lo_ready[Z], at(it, 4, (2, 4)[n // UO]))
                    else:
                        pe.wait_ge(top_ready[Z], at(it, 2 * U, 2 * n - 1))
                    mm(b0, big_ident[:, :], mask[:, Z, m, :], start=True, stop=False)
                    mm(b0, sel_dst[:, h, :], s_own[:, Z, :], start=False, stop=False)
                    mm(b0, s_rows[:, Z, :], sel_src[:, h, :], start=False, stop=True).then_inc(u_ready[Z], 1)
                elif name == "transpose_p":
                    pe.wait_ge(p_ready[Z], at(it, U, n + 1))
                    if 0 < n < H:
                        pe.wait_ge(pt_copied[Z], at(it, U, n))
                    transpose_group(b1, score[:, Z, n % H, :]).then_inc(pt_ready[Z], 1)
                elif name == "mix_heads":
                    if n == 0:
                        pe.wait_ge(pt_copied[Z], at(it, U, H))
                    for h in range(H):
                        m = ((n % 2) * H + h) * (C + 1)
                        last = mm(zbank(Z)[:, n // 2, m:m + C + 1], prob_t[:, Z, h, cols(n)], f1(Z, n, h),
                                  start=True, stop=True)
                    if n == G - 1:
                        last.then_inc(o_ready[Z], 1)
                elif name == "mix":
                    u = (None, UE, UO)[n]
                    pe.wait_ge(pt_copied[Z], at(it, U, u + 1))
                    for g in range(G):
                        m = (g % 2) * (P + 1)
                        last = mm(zbank(Z)[:, g // 2, m:m + P + 1], prob_t[:, Z, u % H, cols(g)],
                                  x2[:, Z, g, :] if u == UE else f3(Z, g), start=True, stop=True)
                    last.then_inc(o_ready[Z], 1)
                elif name == "edge_scores":
                    if n == 0:
                        pe.wait_ge(xt_copied[Z], at(it, 4, 3))
                    else:
                        pe.wait_ge(xs_ready[Z], at(it, K - 1, n))
                    if n == 2:
                        pe.wait_ge(t_ready[Z], at(it, U, UE + 1))
                    if n == 3:
                        pe.wait_ge(e_joined[Z], at(it, K - 1, 1))
                    b = b1 if n % 2 else b0
                    mm(b, big_ident[:, :], mask[:, Z, n, :], start=True, stop=False)
                    for g in range(G):
                        last = mm(b[:, cols(g)], x_t[:, Z, cols(g)], xs_t[:, Z, n, cols(g)], start=False, stop=(g == G - 1))
                    last.then_inc(e_ready[Z], 1)

            part_2_beats(pe, PE_ORDER, step)


_INS = ['x', 'adj', 'L0_gnn_weight', 'L0_gnn_w_ih', 'L0_gnn_w_hh', 'L0_gnn_b_ih', 'L0_gnn_b_hh', 'L1_gnn_W',
        'L1_gnn_b', 'L1_gnn_a', 'L2_gnn_a0', 'L2_gnn_a1', 'L2_gnn_a2', 'L2_gnn_a3', 'L3_gnn_W', 'L3_gnn_a']


def kernel(**inputs):
    import numpy as np
    import concourse.bacc as bacc
    from concourse.bass_utils import run_bass_kernel_spmd

    nc = bacc.Bacc("TRN2", target_bir_lowering=False, num_devices=1)
    arrays, aps = {}, {}
    for name in _INS:
        a = np.ascontiguousarray(inputs[name])
        arrays[f"in_{name}"] = a
        aps[name] = nc.dram_tensor(f"in_{name}", a.shape, mybir.dt.from_np(a.dtype), kind="ExternalInput").ap()
    out = nc.dram_tensor("out_x", inputs["x"].shape, F32, kind="ExternalOutput").ap()
    a = aps
    program(nc, a['x'], a['adj'], a['L0_gnn_weight'], a['L0_gnn_w_ih'], a['L0_gnn_w_hh'], a['L0_gnn_b_ih'],
            a['L0_gnn_b_hh'], a['L1_gnn_W'], a['L1_gnn_b'], a['L1_gnn_a'],
            [a[f'L2_gnn_a{k}'] for k in range(4)], a['L3_gnn_W'], a['L3_gnn_a'], out)
    r = run_bass_kernel_spmd(nc, [arrays], core_ids=[0])
    return r.results[0]["out_x"]
```
